# Optimizing a Trainium2 kernel written in Bass

```python
import numpy as np
import jax
import jax.numpy as jnp

def _softmax(x, axis=-1):
    return jax.nn.softmax(x, axis=axis)

def _gelu(x):
    return jax.nn.gelu(x, approximate=True)

def _silu(x):
    return jax.nn.silu(x)

def _sigmoid(x):
    return jax.nn.sigmoid(x)

def _layernorm(x, axis=-1, eps=1e-05):
    m = jnp.mean(x, axis=axis, keepdims=True)
    v = jnp.var(x, axis=axis, keepdims=True)
    return (x - m) / jnp.sqrt(v + eps)

def _scatter_add(tgt, idx, src, axis=0):
    return tgt.at[idx].add(src)

def _segment_sum(src, seg, n):
    return jax.ops.segment_sum(src, seg, n)
kernel_name = 'mk_seq_preln_d1_jaxref_r4_a7e169'

def setup_inputs(seed: int=0):
    np.random.seed(seed)
    _w = jnp.asarray

    def _L0_attn_setup():
        import jax, jax.numpy as jnp
        import numpy as np
        B, N, E, H = (1, 1024, 512, 16)
        D = E // H
        DEGREE = 4
        LN_EPS = 1e-05
        ROPE_BASE = 10000.0

        def rope_cos_sin(n, d):
            inv_freq = 1.0 / ROPE_BASE ** (jnp.arange(0, d, 2, dtype=jnp.float32) / d)
            t = jnp.arange(n, dtype=jnp.float32)[:, None] * inv_freq[None, :]
            return (jnp.cos(t), jnp.sin(t))

        def apply_rope(x, cos, sin):
            x1, x2 = jnp.split(x, 2, axis=-1)
            c = cos[None, :, None, :]
            s = sin[None, :, None, :]
            return jnp.concatenate([x1 * c - x2 * s, x1 * s + x2 * c], axis=-1)

        def layernorm(x, scale, bias, eps=LN_EPS):
            m = jnp.mean(x, axis=-1, keepdims=True)
            v = jnp.var(x, axis=-1, keepdims=True)
            return (x - m) * jax.lax.rsqrt(v + eps) * scale + bias

        def polynomial_attention(q, k, v, degree, is_causal):
            a = jnp.einsum('bhnd,bhmd->bhnm', q, k) ** degree
            if is_causal:
                a = jnp.tril(a)
            denom = jnp.sum(a, axis=-1, keepdims=True)
            return jnp.einsum('bhnm,bhmd->bhnd', a / denom, v)
        key = jax.random.key(seed)
        k0, k1, k2 = jax.random.split(key, 3)
        x = jax.random.normal(k0, (B, N, E), dtype=jnp.float32)
        w_qkv = jax.random.normal(k1, (E, 3 * E), dtype=jnp.float32) * (1.0 / np.sqrt(E))
        w_out = jax.random.normal(k2, (E, E), dtype=jnp.float32) * (1.0 / np.sqrt(E))
        ln_scale = jnp.ones((D,), dtype=jnp.float32)
        ln_bias = jnp.zeros((D,), dtype=jnp.float32)
        return {'x': x, 'w_qkv': w_qkv, 'w_out': w_out, 'ln_scale': ln_scale, 'ln_bias': ln_bias}
    _L0_attn_in = _L0_attn_setup()

    def _L0_ffn_setup():
        import jax, jax.numpy as jnp
        import numpy as np
        NUM_EXPERTS = 16
        TOP_K = 4
        N_GROUP = 4
        TOPK_GROUP = 2
        SCALING = 2.5

        def _route(x, gate_weight, expert_bias):
            logits = x @ gate_weight.T
            scores = jax.nn.sigmoid(logits)
            biased = scores + expert_bias[None, :]
            T = x.shape[0]
            gsz = NUM_EXPERTS // N_GROUP
            grp = biased.reshape(T, N_GROUP, gsz)
            top2, _ = jax.lax.top_k(grp, 2)
            group_scores = top2.sum(-1)
            _, gidx = jax.lax.top_k(group_scores, TOPK_GROUP)
            gmask = jax.nn.one_hot(gidx, N_GROUP, dtype=scores.dtype).sum(1)
            emask = jnp.repeat(gmask, gsz, axis=1)
            masked = jnp.where(emask > 0, biased, -jnp.inf)
            _, sel = jax.lax.top_k(masked, TOP_K)
            w = jnp.take_along_axis(scores, sel, axis=1)
            w = w / (w.sum(-1, keepdims=True) + 1e-20)
            return (w * SCALING, sel)

        def _moe(x, w, sel, gate_proj, up_proj, down_proj):
            cw = (jax.nn.one_hot(sel, NUM_EXPERTS, dtype=x.dtype) * w[..., None]).sum(1)

            def body(acc, inp):
                g, u, d, we = inp
                y = jax.nn.silu(x @ g.T) * (x @ u.T) @ d.T
                return (acc + we[:, None] * y, None)
            out, _ = jax.lax.scan(body, jnp.zeros_like(x), (gate_proj, up_proj, down_proj, cw.T))
            return out
        key = jax.random.key(seed)
        ks = jax.random.split(key, 9)
        B, S, H, I = (2, 256, 512, 256)
        w = lambda k, shape: jax.random.normal(k, shape, jnp.float32) * 0.02
        return {'hidden_states': jax.random.normal(ks[0], (B, S, H), jnp.float32), 'gate_weight': w(ks[1], (NUM_EXPERTS, H)), 'expert_bias': jnp.zeros((NUM_EXPERTS,), jnp.float32), 'gate_proj': w(ks[2], (NUM_EXPERTS, I, H)), 'up_proj': w(ks[3], (NUM_EXPERTS, I, H)), 'down_proj': w(ks[4], (NUM_EXPERTS, H, I)), 'shared_gate': w(ks[5], (I, H)), 'shared_up': w(ks[6], (I, H)), 'shared_down': w(ks[7], (H, I))}
    _L0_ffn_in = _L0_ffn_setup()
    _d = {'L0_attn_x': _L0_attn_in['x'], 'L0_attn_w_qkv': _L0_attn_in['w_qkv'], 'L0_attn_w_out': _L0_attn_in['w_out'], 'L0_attn_ln_scale': _L0_attn_in['ln_scale'], 'L0_attn_ln_bias': _L0_attn_in['ln_bias'], 'L0_ffn_gate_weight': _L0_ffn_in['gate_weight'], 'L0_ffn_expert_bias': _L0_ffn_in['expert_bias'], 'L0_ffn_gate_proj': _L0_ffn_in['gate_proj'], 'L0_ffn_up_proj': _L0_ffn_in['up_proj'], 'L0_ffn_down_proj': _L0_ffn_in['down_proj'], 'L0_ffn_shared_gate': _L0_ffn_in['shared_gate'], 'L0_ffn_shared_up': _L0_ffn_in['shared_up'], 'L0_ffn_shared_down': _L0_ffn_in['shared_down']}
    _x0 = _d['L0_attn_x']
    _d['L0_attn_x'] = jax.random.normal(jax.random.fold_in(jax.random.key(seed), 1), (4, 512, 512), dtype=_x0.dtype)
    del _x0
    return _d

def reference(L0_attn_x, L0_attn_w_qkv, L0_attn_w_out, L0_attn_ln_scale, L0_attn_ln_bias, L0_ffn_gate_weight, L0_ffn_expert_bias, L0_ffn_gate_proj, L0_ffn_up_proj, L0_ffn_down_proj, L0_ffn_shared_gate, L0_ffn_shared_up, L0_ffn_shared_down):

    def _L0_attn_ref(x, w_qkv, w_out, ln_scale, ln_bias):
        import jax, jax.numpy as jnp
        import numpy as np
        B, N, E, H = (1, 1024, 512, 16)
        D = E // H
        DEGREE = 4
        LN_EPS = 1e-05
        ROPE_BASE = 10000.0

        def rope_cos_sin(n, d):
            inv_freq = 1.0 / ROPE_BASE ** (jnp.arange(0, d, 2, dtype=jnp.float32) / d)
            t = jnp.arange(n, dtype=jnp.float32)[:, None] * inv_freq[None, :]
            return (jnp.cos(t), jnp.sin(t))

        def apply_rope(x, cos, sin):
            x1, x2 = jnp.split(x, 2, axis=-1)
            c = cos[None, :, None, :]
            s = sin[None, :, None, :]
            return jnp.concatenate([x1 * c - x2 * s, x1 * s + x2 * c], axis=-1)

        def layernorm(x, scale, bias, eps=LN_EPS):
            m = jnp.mean(x, axis=-1, keepdims=True)
            v = jnp.var(x, axis=-1, keepdims=True)
            return (x - m) * jax.lax.rsqrt(v + eps) * scale + bias

        def polynomial_attention(q, k, v, degree, is_causal):
            a = jnp.einsum('bhnd,bhmd->bhnm', q, k) ** degree
            if is_causal:
                a = jnp.tril(a)
            denom = jnp.sum(a, axis=-1, keepdims=True)
            return jnp.einsum('bhnm,bhmd->bhnd', a / denom, v)
        b, n, e = x.shape
        proj = x @ w_qkv
        q, k, v = jnp.split(proj, 3, axis=-1)
        q = q.reshape(b, n, H, D)
        k = k.reshape(b, n, H, D)
        v = v.reshape(b, n, H, D)
        cos, sin = rope_cos_sin(n, D)
        q = apply_rope(q, cos, sin)
        k = apply_rope(k, cos, sin)
        q = q.transpose(0, 2, 1, 3)
        k = k.transpose(0, 2, 1, 3)
        v = v.transpose(0, 2, 1, 3)
        q = layernorm(q, ln_scale, ln_bias)
        k = layernorm(k, ln_scale, ln_bias)
        out = polynomial_attention(q, k, v, DEGREE, True)
        out = out.transpose(0, 2, 1, 3).reshape(b, n, e)
        out = out @ w_out
        return out

    def _L0_ffn_ref(hidden_states, gate_weight, expert_bias, gate_proj, up_proj, down_proj, shared_gate, shared_up, shared_down):
        import jax, jax.numpy as jnp
        import numpy as np
        NUM_EXPERTS = 16
        TOP_K = 4
        N_GROUP = 4
        TOPK_GROUP = 2
        SCALING = 2.5

        def _route(x, gate_weight, expert_bias):
            logits = x @ gate_weight.T
            scores = jax.nn.sigmoid(logits)
            biased = scores + expert_bias[None, :]
            T = x.shape[0]
            gsz = NUM_EXPERTS // N_GROUP
            grp = biased.reshape(T, N_GROUP, gsz)
            top2, _ = jax.lax.top_k(grp, 2)
            group_scores = top2.sum(-1)
            _, gidx = jax.lax.top_k(group_scores, TOPK_GROUP)
            gmask = jax.nn.one_hot(gidx, N_GROUP, dtype=scores.dtype).sum(1)
            emask = jnp.repeat(gmask, gsz, axis=1)
            masked = jnp.where(emask > 0, biased, -jnp.inf)
            _, sel = jax.lax.top_k(masked, TOP_K)
            w = jnp.take_along_axis(scores, sel, axis=1)
            w = w / (w.sum(-1, keepdims=True) + 1e-20)
            return (w * SCALING, sel)

        def _moe(x, w, sel, gate_proj, up_proj, down_proj):
            cw = (jax.nn.one_hot(sel, NUM_EXPERTS, dtype=x.dtype) * w[..., None]).sum(1)

            def body(acc, inp):
                g, u, d, we = inp
                y = jax.nn.silu(x @ g.T) * (x @ u.T) @ d.T
                return (acc + we[:, None] * y, None)
            out, _ = jax.lax.scan(body, jnp.zeros_like(x), (gate_proj, up_proj, down_proj, cw.T))
            return out
        B, S, H = hidden_states.shape
        x = hidden_states.reshape(-1, H)
        w, sel = _route(x, gate_weight, expert_bias)
        out = _moe(x, w, sel, gate_proj, up_proj, down_proj)
        shared = jax.nn.silu(x @ shared_gate.T) * (x @ shared_up.T) @ shared_down.T
        return (out + shared).reshape(B, S, H)
    x = L0_attn_x
    x = x + _L0_attn_ref(_layernorm(x, axis=-1), L0_attn_w_qkv, L0_attn_w_out, L0_attn_ln_scale, L0_attn_ln_bias)
    x = x + _L0_ffn_ref(_layernorm(x, axis=-1), L0_ffn_gate_weight, L0_ffn_expert_bias, L0_ffn_gate_proj, L0_ffn_up_proj, L0_ffn_down_proj, L0_ffn_shared_gate, L0_ffn_shared_up, L0_ffn_shared_down)
    return x

_drawn_inputs = setup_inputs


def setup_inputs(seed=0):
    import zlib

    import numpy as np

    out = dict(_drawn_inputs(seed))
    spreads = {'L0_attn_ln_scale': (1.0, 0.2),
     'L0_attn_ln_bias': (0.0, 0.1),
     'L0_ffn_expert_bias': (0.0, 0.1)}
    factors = {}
    for name, (base, spread) in spreads.items():
        noise = np.random.default_rng([zlib.crc32(name.encode()), seed]).standard_normal(out[name].shape)
        drawn = base * np.exp(spread * noise) if base else spread * noise
        out[name] = jnp.asarray(drawn.astype(out[name].dtype))
    for name, factor in factors.items():
        out[name] = (out[name] * factor).astype(out[name].dtype)
    return out
```

```python
from contextlib import ExitStack

import numpy as np

import concourse.bass as bass
from concourse import mybir

F32 = mybir.dt.float32
F16 = mybir.dt.float16
I32 = mybir.dt.int32
ALU = mybir.AluOpType
ACT = mybir.ActivationFunctionType
AX_X = mybir.AxisListType.X

P = 128
B, N, E = 4, 512, 512
H, D = 16, 32
HG = P // D
NG = H // HG
T = B * N
MB = N // P
EC = E // P
NX, TOPK, NGR, GTOP = 16, 4, 4, 2
GSZ = NX // NGR
FF = 256
FC = FF // P
ROUTE_SCALE = 2.5
EPS = 1e-5
TB = T // P
RT = T * TOPK // P + NX
NT = TB + RT
JB = T // P
NCOL = NX * JB
CH = NCOL // P
NEG = 1.0e30


class Tile:

    def __init__(self, r, lo):
        self.r, self.lo, self.par = r, lo, lo % 2

    def at(self, d=0):
        return self.lo + d if self.r is None else self.r * 2 + (self.lo + d)

    def plus(self, d):
        return Tile(self.r, self.lo + d)

    def uses(self, d=0):
        return self.lo // 2 + 1 + d if self.r is None else self.r + (self.lo // 2 + 1 + d)

    def is_(self, n):
        return self.r is None and self.lo == n

    def below(self, n):
        return self.r is None and self.lo < n


def tile_pairs(eng, lo, hi, step):
    with eng.Fori(0, (hi - lo) // 2) as r:
        step(Tile(r, lo))
        step(Tile(r, lo + 1))


def constants():
    c = {}
    inv = (1.0 / np.float32(10000.0) ** (np.arange(0, D, 2, dtype=np.float32) / np.float32(D))).astype(np.float32)
    t = np.arange(N, dtype=np.float32)[:, None] * inv[None, :]
    cos, sin = np.cos(t).astype(np.float32), np.sin(t).astype(np.float32)
    lay = lambda a: a.reshape(MB, P, D).transpose(1, 0, 2)
    c["rope_cos"] = lay(np.concatenate([cos, cos], 1))
    c["rope_sin"] = lay(np.concatenate([-sin, sin], 1))
    c["ident"] = np.eye(P)
    i = np.arange(P)
    c["causal"] = i[:, None] <= i[None, :]
    c["before"] = i[:, None] < i[None, :]
    e = np.arange(NX)
    c["tie16"] = np.tile((e[None, :] < e[:, None]).reshape(1, NX * NX), (P, 1))
    g = np.arange(NGR)
    c["tie4"] = np.tile((g[None, :] < g[:, None]).reshape(1, NGR * NGR), (P, 1))
    c["iota"] = np.tile(np.arange(NCOL)[None, :], (P, 1))
    col = np.arange(NCOL).reshape(CH, P).T
    c["col_piece"] = col % JB
    c["col_onehot"] = (col // JB)[:, :, None] == e[None, None, :]
    c["col_id"] = np.repeat((col // JB + 1)[:, :, None], P, 2)
    c["token"] = np.arange(T).reshape(TB, P).T
    return {k: np.ascontiguousarray(v.reshape(P, -1).astype(np.float32)) for k, v in c.items()}


def build(nc, x, w_qkv, w_out, ln_scale, ln_bias, gate_w, expert_bias, w_gu, w_dn, cst, out):
    ctx = ExitStack()
    with ctx:
        sb = lambda n, s, d=F32: ctx.enter_context(nc.sbuf_tensor(n, s, d))
        sem = lambda n: ctx.enter_context(nc.semaphore(n))

        x1_dram = nc.dram_tensor("x1_scratch", [TB, P, E], F32, kind="Internal").ap()
        xn_dram = nc.dram_tensor("xn_scratch", [T, E], F32, kind="Internal").ap()
        y_dram = nc.dram_tensor("y_scratch", [NT * P, E], F32, kind="Internal").ap()

        EW = EC * 2 * FF
        arena = sb("arena", [P, (NX + 1) * EW])
        EARLY = 9
        top = [EARLY * EW]

        def over(shape):
            n = int(np.prod(shape))
            a = arena[:, top[0]:top[0] + n]
            top[0] += n
            assert top[0] <= (NX + 1) * EW
            return a.rearrange("p (a b) -> p a b", a=shape[0]) if len(shape) == 2 else a

        gu = arena[:].rearrange("p (e c n) -> p e c n", e=NX + 1, c=EC)
        wqkv = over([EC, 3 * E])
        wout = over([EC, E])
        xnT = over([EC, N])
        qT = over([NG, N])
        kT = over([NG, N])
        s_sq = over([HG, N])
        C = {k: sb("c_" + k, [P, v.shape[1]]) for k, v in cst.items()}
        ident = C["ident"][:]
        ln_s, ln_b = sb("ln_s", [P, 1]), sb("ln_b", [P, 1])
        eps = sb("eps", [P, 1])
        ones = sb("ones", [P, P])
        gwT = sb("gwT", [P, EC, NX])
        ebias = sb("ebias", [P, NX])
        onehot = sb("onehot", [P, TB, TOPK, NX])
        cw = sb("cw", [P, TB, TOPK])
        pos = sb("pos", [P, TB, TOPK])
        slot_tab = sb("slot_tab", [P, CH, P])
        seen = sb("seen", [P, MB + 1, NX])
        row_id = sb("row_id", [P, NT], I32)
        expert_id = sb("expert_id", [P, NT], I32)
        slot_id = sb("slot_id", [P, TB, TOPK], I32)
        oh4 = sb("oh4", [P, MB * TOPK * NX])
        tmp4 = sb("tmp4", [P, MB])
        tile_hot = sb("tile_hot", [P, CH, RT])
        d16, d16i, d2 = sb("d16", [P, 2, NX]), sb("d16i", [P, 2, NX], I32), sb("d2", [P, 3, CH])
        sl = sb("sl", [P, TB, TOPK])
        att = ExitStack()
        sa = lambda n, s, d=F32: att.enter_context(nc.sbuf_tensor(n, s, d))
        xin = sa("xin", [P, MB, E])
        xres = sa("xres", [P, MB, E])
        vtok = sa("vtok", [P, MB, E])
        t1 = sa("t1", [P, 2 * E])
        t2 = sa("t2", [P, 2 * E])
        qkn = sa("qkn", [P, 2 * E])
        s_p4 = sa("s_p4", [P, 2, HG, N])
        st = sa("st", [P, MB, 6])
        mv = sa("mv", [P, MB, 2])
        sd = sa("sd", [P, MB])
        hs = sa("hs", [P, 3, 2 * H])
        rec = t2[:, 0:N]
        xn2 = xin
        attT = xnT
        x2T = t1[:].rearrange("p (k c n) -> p k c n", k=2, c=EC)
        sc, bi, mb, rank, ws = (sa(n, [P, MB, NX]) for n in ("sc", "bi", "mb", "rank", "ws"))
        sel = sa("sel", [P, MB, NX])
        gp = sa("gp", [P, 8, MB * NGR * 2])
        ek = sa("ek", [P, MB, TOPK])
        ki = sa("ki", [P, 3, MB * TOPK], I32)
        kf = sa("kf", [P, 2, MB * TOPK])
        tok4 = sa("tok4", [P, MB])
        cmp1 = qkn[:, 0:MB * NX * NX]
        cmp2 = t2[:, 0:MB * NX * NX]
        ra = s_p4[:].rearrange("p a b n -> p (a b n)")[:, 0:MB * TOPK * P // 2].bitcast(F16).rearrange(
            "p (i r) -> p i r", i=MB * TOPK)
        rb = s_p4[:].rearrange("p a b n -> p (a b n)")[:, 1024:1024 + MB * TOPK * NCOL // 2].bitcast(F16).rearrange(
            "p (i c) -> p i c", i=MB * TOPK)
        att.close()
        moe = ExitStack()
        sm = lambda n, s, d=F32: moe.enter_context(nc.sbuf_tensor(n, s, d))
        xg = sm("xg", [P, 2, E])
        gidx = sm("gidx", [P, 2], I32)
        xgT = sm("xgT", [P, 2, EC, P])
        wd = sm("wd", [P, 2, FC, E])
        sg = sm("sg", [P, 2, FF])
        hh = sm("hh", [P, 2, FF])
        hT = sm("hT", [P, 2, FC, P])
        yy = sm("yy", [P, 2, E])
        fin = sm("fin", [P, 2, 2, E])
        gath = sm("gath", [P, 2, TOPK, E])
        cidx = sm("cidx", [P, 2, TOPK], I32)
        ccw = sm("ccw", [P, 2, TOPK])
        moe.close()

        bank = [ctx.enter_context(nc.psum_tensor(f"bank{i}", [P, 512], F32)) for i in range(8)]
        quad = lambda bk: bk[:].rearrange("p (c n) -> p c n", c=4)

        consts_in, wqkv_in, wout_in, early_in, late_in = map(sem, ("consts_in", "wqkv_in", "wout_in", "early_in", "late_in"))
        xin_in, xres_in, x1_out, xn2_out = map(sem, ("xin_in", "xres_in", "x1_out", "xn2_out"))
        memset_done = sem("memset_done")
        var1, std1, xn_ready = sem("var1"), sem("std1"), sem("xn_ready")
        xT_ps, xT_sb, qkv_ps = sem("xT_ps"), sem("xT_sb"), sem("qkv_ps")
        rope_parts, rotated, mean_ready, centred, squares, hvar, hstd, hrstd, qkn_ready = map(sem, (
            "rope_parts", "rotated", "mean_ready", "centred", "squares", "hvar", "hstd", "hrstd", "qkn_ready"))
        v_sb, qkT_ps, qkT_sb = sem("v_sb"), sem("qkT_ps"), sem("qkT_sb")
        scores_ps, sq_done, p4_done, p4_masked, pv_done, att_done = map(sem, (
            "scores_ps", "sq_done", "p4_done", "p4_masked", "pv_done", "att_done"))
        proj_ps, x1_ready, var2, std2, xn2_ready = map(sem, ("proj_ps", "x1_ready", "var2", "std2", "xn2_ready"))
        x2T_ps, x2T_sb, logits_ps, scores_sig, sel_ready, pos_ps, ab_ready, tab_ps = map(sem, (
            "x2T_ps", "x2T_sb", "logits_ps", "scores_sig", "sel_ready", "pos_ps", "ab_ready", "tab_ps"))
        count_ps, tiles_known, ids_ps, ids_ready, slots_ready = map(sem, (
            "count_ps", "tiles_known", "ids_ps", "ids_ready", "slots_ready"))
        shared_ids, chain = sem("shared_ids"), sem("chain")
        xg_in = [sem("xg_in0"), sem("xg_in1")]
        wd_in = [sem("wd_in0"), sem("wd_in1")]
        y_out = [sem("y_out0"), sem("y_out1")]
        gT_ps, gT_sb, gu_ps, silu_done, h_ready, hT_ps, hT_sb, y_ps, y_sb = map(sem, (
            "gT_ps", "gT_sb", "gu_ps", "silu_done", "h_ready", "hT_ps", "hT_sb", "y_ps", "y_sb"))
        fin_in = [sem("fin_in0"), sem("fin_in1")]
        gath_in = [sem("gath_in0"), sem("gath_in1")]
        fin_out = [sem("fin_out0"), sem("fin_out1")]
        ccw_ready, fin_ready = sem("ccw_ready"), sem("fin_ready")
        NCST = len(cst) + 6

        block = ctx.enter_context(nc.Block())

        def over_tiles(eng, step, first_routed=lambda: None):
            for t in range(3):
                step(Tile(None, t))
            tile_pairs(eng, 3, TB - 1, step)
            step(Tile(None, TB - 1))
            first_routed()
            step(Tile(None, TB))
            tile_pairs(eng, TB + 1, NT - 1, step)
            step(Tile(None, NT - 1))

        @block.sync
        def _(sp):
            sp.dma_start(xin[:], x[0]).then_inc(xin_in, 16)
            for k, v in cst.items():
                sp.dma_start(C[k][:], v).then_inc(consts_in, 16)
            for j in range(HG):
                if j < 2:
                    sp.dma_start(ln_s[64 * j:64 * j + 64, :], ln_scale[64 * j:64 * j + 64, :]).then_inc(consts_in, 16)
                else:
                    sp.dma_start(ln_b[64 * j - 128:64 * j - 64, :], ln_bias[64 * j - 128:64 * j - 64, :]).then_inc(consts_in, 16)
            sp.dma_start(gwT[:], gate_w).then_inc(consts_in, 16)
            sp.dma_start(ebias[:], expert_bias).then_inc(consts_in, 16)
            sp.dma_start(wqkv, w_qkv).then_inc(wqkv_in, 16)
            sp.dma_start(xres[:], x[0]).then_inc(xres_in, 16)
            sp.dma_start(wout, w_out).then_inc(wout_in, 16)
            for e in range(EARLY):
                sp.dma_start(gu[:, e], w_gu[e]).then_inc(early_in, 16)
            for b in range(B):
                sp.wait_ge(x1_ready, MB * (b + 1))
                sp.dma_start(x1_dram[MB * b:MB * b + MB].rearrange("m p e -> p m e"), xres[:]).then_inc(x1_out, 16)
                sp.wait_ge(xn2_ready, MB * (b + 1))
                sp.dma_start(xn_dram[N * b:N * b + N].rearrange("(m p) e -> p m e", p=P), xn2[:]).then_inc(xn2_out, 16)
                if b + 1 < B:
                    sp.wait_ge(xn2_out, 16 * (b + 1))
                    sp.wait_ge(x2T_ps, MB * (b + 1))
                    sp.dma_start(xin[:], x[b + 1]).then_inc(xin_in, 16)
                    sp.wait_ge(x1_out, 16 * (b + 1))
                    sp.dma_start(xres[:], x[b + 1]).then_inc(xres_in, 16)
            sp.wait_ge(proj_ps, MB * B)
            sp.wait_ge(tab_ps, B)
            for e in range(EARLY, NX + 1):
                sp.dma_start(gu[:, e], w_gu[e]).then_inc(late_in, 16)
            sp.wait_ge(x1_out, 16 * B)
            sp.wait_ge(xn2_out, 16 * B)
            sp.wait_ge(shared_ids, 1)

            def store(t):
                k = t.par
                sp.wait_ge(y_sb, t.at(1))
                sp.dma_start(y_dram[bass.ds(t.at() * P, P), :], yy[:, k]).then_inc(y_out[k], 16)

            def load(t):
                k = t.par
                if not t.below(2):
                    sp.wait_ge(y_ps, t.at(-1))
                e = sp.value_load(expert_id[0:1, bass.ds(t.at(), 1)], min_val=0, max_val=NX)
                sp.dma_start(wd[:, k].rearrange("p c n -> p (c n)"), w_dn[bass.ds(e * P, P), :]).then_inc(wd_in[k], 16)

            load(Tile(None, 0))

            def step(t):
                k = t.par
                if t.is_(NT - 1):
                    store(t)
                    return
                load(t.plus(1))
                store(t)

            step(Tile(None, 0))
            tile_pairs(sp, 1, TB - 1, step)
            sp.wait_ge(ids_ready, 1)
            tile_pairs(sp, TB - 1, NT - 1, step)
            step(Tile(None, NT - 1))
            for k in range(2):
                sp.wait_ge(y_out[k], 16 * NT // 2)
            o = out.rearrange("b (m p) e -> (b m) p e", p=P)

            def comb_in(m, k):
                sp.dma_start(fin[:, k, 0], x1_dram[bass.ds(m, 1)].rearrange("m p e -> p (m e)")).then_inc(fin_in[k], 16)
                sp.dma_start(fin[:, k, 1], y_dram[bass.ds(m * P, P), :]).then_inc(fin_in[k], 16)

            def comb_out(m, k):
                sp.wait_ge(fin_ready, m + 1)
                sp.dma_start(o[bass.ds(m, 1)].rearrange("m p e -> p (m e)"), fin[:, k, 0]).then_inc(fin_out[k], 16)
            comb_in(0, 0)
            comb_in(1, 1)
            with sp.Fori(0, TB // 2 - 1) as r:
                for k in range(2):
                    comb_out(2 * r + k, k)
                    sp.wait_ge(fin_out[k], 16 * r + 16)
                    comb_in(2 * r + k + 2, k)
            for k in range(2):
                comb_out(TB - 2 + k, k)
            for k in range(2):
                sp.wait_ge(fin_out[k], 16 * TB // 2)

        @block.tensor
        def _(pe):
            pe.wait_ge(consts_in, 16 * NCST)
            pe.wait_ge(memset_done, 1)
            with pe.Fori(0, B) as b:
                for m in range(MB):
                    pe.wait_ge(xn_ready, b * MB + (m + 1))
                    if m >= 2:
                        pe.wait_ge(xT_sb, b * MB + (m - 1))
                    for c in range(EC):
                        mm = pe.transpose(quad(bank[4 + m % 2])[:, c], xin[:, m, c * P:c * P + P], ident)
                    mm.then_inc(xT_ps, 1)
                pe.wait_ge(wqkv_in, 16)

                def qk_transposes(m):
                    pe.wait_ge(qkn_ready, b * MB + (m + 1))
                    if m:
                        pe.wait_ge(qkT_sb, b * (2 * MB) + 2 * m)
                    for w in range(2):
                        for g in range(NG):
                            mm = pe.transpose(quad(bank[6 + w])[:, g], qkn[:, w * E + g * P:w * E + g * P + P], ident)
                        mm.then_inc(qkT_ps, 1)

                for m in range(MB):
                    pe.wait_ge(xT_sb, b * MB + (m + 1))
                    for w in range(3):
                        if m:
                            pe.wait_ge(*((rope_parts, b * MB + m) if w < 2 else (v_sb, b * MB + m)))
                        for c in range(EC):
                            mm = pe.matmul(bank[w][:], xnT[:, c, m * P:m * P + P], wqkv[:, c, w * E:w * E + E],
                                           start=(c == 0), stop=(c == EC - 1))
                        mm.then_inc(qkv_ps, 1)
                    if m:
                        qk_transposes(m - 1)
                qk_transposes(MB - 1)
                pe.wait_ge(qkT_sb, b * (2 * MB) + 2 * MB)
                pe.wait_ge(v_sb, b * MB + MB)
                for i in range(NG * MB + 1):
                    if i < NG * MB:
                        g, kb = divmod(i, MB)
                        for j in range(HG):
                            if i:
                                pe.wait_ge(sq_done, b * (NG * MB * HG) + (HG * (i - 1) + j + 1))
                            r = slice(D * j, D * j + D)
                            pe.matmul(bank[j][:, 0:N - P * kb], kT[r, g, P * kb:P * kb + P], qT[r, g, P * kb:N],
                                      start=True, stop=True).then_inc(scores_ps, 1)
                    if i:
                        g, kb = divmod(i - 1, MB)
                        if kb == 0 and g:
                            pe.wait_ge(att_done, b * NG + g)
                        for j in range(HG):
                            pe.wait_ge(p4_masked, b * (NG * MB * HG) + (HG * (i - 1) + j + 1))
                            r = slice(D * j, D * j + D)
                            p4 = s_p4[:, (i - 1) % 2, j, 0:N - P * kb]
                            pe.matmul(bank[6][r, P * kb:N], vtok[:, kb, (g * HG + j) * D:(g * HG + j) * D + D], p4,
                                      start=(kb == 0), stop=(kb == MB - 1), skip_group_check=True)
                            mm = pe.matmul(bank[7][r, P * kb:N], ones[:, 0:D], p4,
                                           start=(kb == 0), stop=(kb == MB - 1), skip_group_check=True)
                        mm.then_inc(pv_done, 1)
                pe.wait_ge(wout_in, 16)
                pe.wait_ge(att_done, b * NG + NG)
                for m in range(MB):
                    for g in range(NG):
                        mm = pe.matmul(bank[m][:], attT[:, g, m * P:m * P + P], wout[:, g, :],
                                       start=(g == 0), stop=(g == NG - 1))
                    mm.then_inc(proj_ps, 1)
                def logits(m):
                    pe.wait_ge(x2T_sb, b * MB + (m + 1))
                    for c in range(EC):
                        mm = pe.matmul(bank[6][:, m * NX:m * NX + NX], x2T[:, m % 2, c, :], gwT[:, c, :],
                                       start=(c == 0), stop=(c == EC - 1))
                    return mm
                for m in range(MB):
                    pe.wait_ge(xn2_ready, b * MB + (m + 1))
                    if m >= 2:
                        pe.wait_ge(x2T_sb, b * MB + (m - 1))
                    for c in range(EC):
                        mm = pe.transpose(quad(bank[4 + m % 2])[:, c], xn2[:, m, c * P:c * P + P], ident)
                    mm.then_inc(x2T_ps, 1)
                    if m:
                        logits(m - 1)
                logits(MB - 1).then_inc(logits_ps, 1)
                pe.wait_ge(sel_ready, b + 1)
                for m in range(MB):
                    o = bank[7][:, m * NX:m * NX + NX]
                    pe.matmul(o, C["before"][:], sel[:, m, :], start=True, stop=False)
                    mm = pe.matmul(o, ones[:], seen[:, m, :], start=False, stop=True)
                mm.then_inc(pos_ps, 1)
                pe.wait_ge(ab_ready, b + 1)
                for h in range(CH):
                    for i in range(MB * TOPK):
                        mm = pe.matmul(bank[6][:, h * P:h * P + P], rb[:, i, h * P:h * P + P], ra[:, i, :],
                                       start=(i == 0), stop=(i == MB * TOPK - 1))
                mm.then_inc(tab_ps, 1)
            pe.wait_ge(sel_ready, B + 1)
            pe.matmul(bank[7][:, 0:NX], ones[:], seen[:, 0, :], start=True, stop=True).then_inc(count_ps, 1)

            def gather_T(t):
                k = t.par
                pe.wait_ge(xg_in[k], t.uses() * 16)
                if not t.below(2):
                    pe.wait_ge(gT_sb, t.at(-1))
                for c in range(EC):
                    mm = pe.transpose(quad(bank[k])[:, c], xg[:, k, c * P:c * P + P], ident)
                mm.then_inc(gT_ps, 1)

            def gate_up(t, e):
                k = t.par
                pe.wait_ge(gT_sb, t.at(1))
                if not t.below(2):
                    pe.wait_ge(h_ready, t.at(-1))
                for c in range(EC):
                    w = gu[:, 0, c, :] if e is None else gu[:, bass.ds(e, 1), c, :]
                    mm = pe.matmul(bank[2 + k][:], xgT[:, k, c, :], w, start=(c == 0), stop=(c == EC - 1))
                mm.then_inc(gu_ps, 1)

            def down(t):
                k = t.par
                pe.wait_ge(h_ready, t.at(1))
                if not t.below(1):
                    pe.wait_ge(hT_sb, t.at())
                for c in range(FC):
                    mm = pe.transpose(bank[4][:, c * P:c * P + P], hh[:, k, c * P:c * P + P], ident)
                mm.then_inc(hT_ps, 1)
                pe.wait_ge(hT_sb, t.at(1))
                pe.wait_ge(wd_in[k], t.uses() * 16)
                if not t.below(2):
                    pe.wait_ge(y_sb, t.at(-1))
                for c in range(FC):
                    mm = pe.matmul(bank[5 + k][:], hT[:, k, c, :], wd[:, k, c, :], start=(c == 0), stop=(c == FC - 1))
                mm.then_inc(y_ps, 1)

            def step(t, routed):
                k = t.par
                e = pe.value_load(expert_id[0:1, bass.ds(t.at(), 1)], min_val=0, max_val=NX) if routed else None
                if not t.is_(NT - 1):
                    gather_T(t.plus(1))
                gate_up(t, e)
                if not t.is_(0):
                    down(t.plus(-1))

            pe.wait_ge(early_in, 16 * EARLY)
            gather_T(Tile(None, 0))
            for t in range(3):
                step(Tile(None, t), False)
            tile_pairs(pe, 3, TB - 3, lambda t: step(t, False))
            pe.wait_ge(tiles_known, 1)
            for h in range(CH):
                pe.matmul(bank[7][:, 0:RT], slot_tab[:, h, :], tile_hot[:, h, :], start=(h == 0), stop=(h == CH - 1))
            for h in range(CH):
                mm = pe.matmul(bank[7][:, RT:2 * RT], C["col_id"][:, h * P:h * P + P], tile_hot[:, h, :],
                               start=(h == 0), stop=(h == CH - 1))
            mm.then_inc(ids_ps, 1)
            step(Tile(None, TB - 3), False)
            step(Tile(None, TB - 2), False)
            step(Tile(None, TB - 1), False)
            pe.wait_ge(late_in, 16 * (NX + 1 - EARLY))
            pe.wait_ge(ids_ready, 1)
            tile_pairs(pe, TB, NT - 2, lambda t: step(t, True))
            step(Tile(None, NT - 2), True)
            step(Tile(None, NT - 1), True)
            down(Tile(None, NT - 1))

        @block.scalar
        def _(act):
            act.wait_ge(consts_in, 16 * NCST)
            act.wait_ge(memset_done, 1)
            with act.Fori(0, B) as b:
                act.wait_ge(var1, b + 1)
                act.activation(sd[:], mv[:, :, 1], ACT.Sqrt, bias=eps[:, 0:1]).then_inc(std1, 1)
                for m in range(MB):
                    act.wait_ge(xT_ps, b * MB + (m + 1))
                    act.activation(xnT[:, :, m * P:m * P + P], quad(bank[4 + m % 2]), ACT.Copy).then_inc(xT_sb, 1)

                def qkT(m):
                    for w, dst in enumerate((qT, kT)):
                        act.wait_ge(qkT_ps, b * (2 * MB) + (2 * m + w + 1))
                        act.activation(dst[:, :, m * P:m * P + P], quad(bank[6 + w]), ACT.Identity,
                                       bias=ln_b[:, 0:1], scale=ln_s[:, 0:1]).then_inc(qkT_sb, 1)

                for m in range(MB):
                    act.wait_ge(qkv_ps, b * (3 * MB) + (3 * m + 3))
                    act.activation(vtok[:, m, :], bank[2][:], ACT.Copy).then_inc(v_sb, 1)
                    act.wait_ge(centred, b * MB + (m + 1))
                    act.activation(t2[:], t1[:], ACT.Square).then_inc(squares, 1)
                    act.wait_ge(hvar, b * MB + (m + 1))
                    act.activation(hs[:, 1, :], hs[:, 0, :], ACT.Sqrt, bias=eps[:, 0:1], scale=1.0 / D).then_inc(hstd, 1)
                    if m:
                        qkT(m - 1)
                qkT(MB - 1)
                for i in range(NG * MB):
                    kb = i % MB
                    for j in range(HG):
                        n = HG * i + j
                        act.wait_ge(scores_ps, b * (NG * MB * HG) + (n + 1))
                        if i:
                            act.wait_ge(p4_done, b * (NG * MB * HG) + (n - HG + 1))
                        act.activation(s_sq[:, j, 0:N - P * kb], bank[j][:, 0:N - P * kb], ACT.Square).then_inc(sq_done, 1)
                act.wait_ge(var2, b + 1)
                act.activation(sd[:], mv[:, :, 1], ACT.Sqrt, bias=eps[:, 0:1]).then_inc(std2, 1)
                for m in range(MB):
                    act.wait_ge(x2T_ps, b * MB + (m + 1))
                    act.activation(x2T[:, m % 2], quad(bank[4 + m % 2]), ACT.Copy).then_inc(x2T_sb, 1)
                act.wait_ge(logits_ps, b + 1)
                act.activation(sc[:].rearrange("p m e -> p (m e)"), bank[6][:, 0:MB * NX], ACT.Sigmoid).then_inc(scores_sig, 1)
            def copy_T(t):
                k = t.par
                act.wait_ge(gT_ps, t.at(1))
                if not t.below(2):
                    act.wait_ge(gu_ps, t.at(-1))
                act.activation(xgT[:, k], quad(bank[k]), ACT.Copy).then_inc(gT_sb, 1)

            def step(t):
                k = t.par
                if not t.is_(NT - 1):
                    copy_T(t.plus(1))
                act.wait_ge(gu_ps, t.at(1))
                if not t.below(2):
                    act.wait_ge(h_ready, t.at(-1))
                act.activation(sg[:, k], bank[2 + k][:, 0:FF], ACT.Silu).then_inc(silu_done, 1)

            act.wait_ge(ab_ready, B)
            copy_T(Tile(None, 0))
            over_tiles(act, step)

        @block.gpsimd
        def _(pool):
            pool.memset(ones[:], 1.0)
            pool.memset(seen[:, 0, :], 0.0)
            pool.memset(slot_tab[:], 0.0)
            pool.memset(eps[:], EPS)
            pool.memset(expert_id[:, 0:TB], 0)
            pool.drain()
            pool.memset(tile_hot[:], 0.0).then_inc(memset_done, 1)
            pool.wait_ge(consts_in, 16 * NCST)
            pool.tensor_copy(row_id[:, 0:TB], C["token"][:]).then_inc(shared_ids, 1)
            heads = lambda a: a.rearrange("p (h d) -> p h d", d=D)
            per_head = lambda a: a.unsqueeze(2).to_broadcast([P, 2 * H, D])
            with pool.Fori(0, B) as b:
                for m in range(MB):
                    pool.wait_ge(rope_parts, b * MB + (m + 1))
                    pool.tensor_tensor(t1[:], t1[:], t2[:], ALU.add).then_inc(rotated, 1)
                    pool.wait_ge(mean_ready, b * MB + (m + 1))
                    pool.tensor_tensor(heads(t1[:]), heads(t1[:]), per_head(hs[:, 0, :]), ALU.subtract).then_inc(centred, 1)
                    pool.wait_ge(hrstd, b * MB + (m + 1))
                    if m:
                        pool.wait_ge(qkT_ps, b * (2 * MB) + 2 * m)
                    pool.tensor_tensor(heads(qkn[:]), heads(t1[:]), per_head(hs[:, 2, :]), ALU.mult).then_inc(qkn_ready, 1)
                for n in range(NG * MB * HG):
                    pool.wait_ge(p4_done, b * (NG * MB * HG) + (n + 1))
                    d = s_p4[:, (n // HG) % 2, n % HG, 0:P]
                    pool.tensor_tensor(d, d, C["causal"][:], ALU.mult).then_inc(p4_masked, 1)

            def step(t):
                k = t.par
                if not t.below(2):
                    pool.wait_ge(gT_ps, t.at(-1))
                pool.tensor_copy(gidx[:, k:k + 1], row_id[:, bass.ds(t.at(), 1)])
                pool.drain()
                pool.indirect_dma_start(out=xg[:, k], out_offset=None, in_=xn_dram,
                                        in_offset=bass.IndirectOffsetOnAxis(ap=gidx[:, k:k + 1], axis=0)
                                        ).then_inc(xg_in[k], 16)
            pool.wait_ge(ab_ready, B)
            pool.wait_ge(xn2_out, 16 * B)
            pool.wait_ge(x1_out, 16 * B)
            pool.wait_ge(tab_ps, B)
            over_tiles(pool, step, lambda: pool.wait_ge(ids_ready, 1))

            pool.wait_ge(slots_ready, 1)
            for k in range(2):
                pool.wait_ge(y_out[k], 16 * NT // 2)

            def comb(m, k):
                pool.tensor_copy(cidx[:, k], slot_id[:, bass.ds(m, 1), :].rearrange("p a k -> p (a k)"))
                pool.tensor_copy(ccw[:, k], cw[:, bass.ds(m, 1), :].rearrange("p a k -> p (a k)")).then_inc(ccw_ready, 1)
                pool.drain()
                for c in range(TOPK):
                    pool.indirect_dma_start(out=gath[:, k, c], out_offset=None, in_=y_dram,
                                            in_offset=bass.IndirectOffsetOnAxis(ap=cidx[:, k, c:c + 1], axis=0)
                                            ).then_inc(gath_in[k], 16)
            comb(0, 0)
            comb(1, 1)
            with pool.Fori(1, TB // 2) as r:
                for k in range(2):
                    pool.wait_ge(fin_ready, r * 2 + (k - 1))
                    comb(2 * r + k, k)

        @block.vector
        def _(dve):
            dve.wait_ge(consts_in, 16 * NCST)
            dve.wait_ge(memset_done, 1)
            heads = lambda a: a.rearrange("p (h d) -> p h d", d=D)

            def norm_stats(m, src, last):
                dve.bn_stats(st[:, m, :], src[:, m, :])
                if last is not None:
                    dve.drain()
                    for k in range(MB):
                        i = dve.bn_aggr(mv[:, k, :], st[:, k, :])
                    i.then_inc(last, 1)

            def normed(dst, src, ready):
                dve.reciprocal(sd[:], sd[:])
                dve.drain()
                for m in range(MB):
                    dve.tensor_scalar(dst[:, m, :], src[:, m, :], mv[:, m, 0:1], sd[:, m:m + 1],
                                      ALU.subtract, ALU.mult).then_inc(ready, 1)

            with dve.Fori(0, B) as b:
                dve.wait_ge(xin_in, b * 16 + 16)
                for m in range(MB):
                    norm_stats(m, xin, var1 if m == MB - 1 else None)
                dve.wait_ge(std1, b + 1)
                normed(xin, xin, xn_ready)
                for m in range(MB):
                    dve.wait_ge(qkv_ps, b * (3 * MB) + (3 * m + 2))
                    if m:
                        dve.wait_ge(qkn_ready, b * MB + m)
                    cos = C["rope_cos"][:, m * D:m * D + D].unsqueeze(1).to_broadcast([P, H, D])
                    for w in range(2):
                        ps, a1, a2 = heads(bank[w][:]), heads(t1[:, w * E:w * E + E]), heads(t2[:, w * E:w * E + E])
                        dve.tensor_tensor(a1, ps, cos, ALU.mult)
                        for h in range(2):
                            lo, hi = h * D // 2, (1 - h) * D // 2
                            sin = C["rope_sin"][:, m * D + lo:m * D + lo + D // 2].unsqueeze(1).to_broadcast([P, H, D // 2])
                            i = dve.tensor_tensor(a2[:, :, lo:lo + D // 2], ps[:, :, hi:hi + D // 2], sin, ALU.mult)
                    i.then_inc(rope_parts, 1)
                    dve.wait_ge(rotated, b * MB + (m + 1))
                    dve.tensor_reduce(hs[:, 0, :], heads(t1[:]), AX_X, ALU.add)
                    dve.drain()
                    dve.tensor_scalar(hs[:, 0, :], hs[:, 0, :], 1.0 / D, None, ALU.mult).then_inc(mean_ready, 1)
                    dve.wait_ge(squares, b * MB + (m + 1))
                    dve.tensor_reduce(hs[:, 0, :], heads(t2[:]), AX_X, ALU.add).then_inc(hvar, 1)
                    dve.wait_ge(hstd, b * MB + (m + 1))
                    dve.reciprocal(hs[:, 2, :], hs[:, 1, :]).then_inc(hrstd, 1)

                def finish(g):
                    dve.wait_ge(pv_done, b * (NG * MB) + (g * MB + MB))
                    dve.reciprocal(rec, bank[7][:])
                    dve.drain()
                    dve.tensor_tensor(attT[:, g, :], bank[6][:], rec, ALU.mult).then_inc(att_done, 1)

                for i in range(NG * MB):
                    kb = i % MB
                    if i >= 2:
                        dve.wait_ge(pv_done, b * (NG * MB) + (i - 1))
                    for j in range(HG):
                        dve.wait_ge(sq_done, b * (NG * MB * HG) + (HG * i + j + 1))
                        s2 = s_sq[:, j, 0:N - P * kb]
                        dve.tensor_tensor(s_p4[:, i % 2, j, 0:N - P * kb], s2, s2, ALU.mult).then_inc(p4_done, 1)
                    if i and kb == 0:
                        finish(i // MB - 1)
                finish(NG - 1)
                dve.wait_ge(xres_in, b * 16 + 16)
                for m in range(MB):
                    dve.wait_ge(proj_ps, b * MB + (m + 1))
                    dve.tensor_tensor(xres[:, m, :], xres[:, m, :], bank[m][:], ALU.add).then_inc(x1_ready, 1)
                dve.drain()
                for m in range(MB):
                    norm_stats(m, xres, var2 if m == MB - 1 else None)
                dve.wait_ge(std2, b + 1)
                normed(xn2, xres, xn2_ready)
                fl = lambda a: a.rearrange("p m e -> p (m e)")
                dve.tensor_copy(tok4[:], C["token"][:, bass.ds(b * MB, MB)])
                dve.wait_ge(scores_sig, b + 1)
                dve.tensor_tensor(bi[:], sc[:], ebias[:].unsqueeze(1).to_broadcast([P, MB, NX]), ALU.add)
                dve.drain()
                pr = fl(bi[:]).rearrange("p (g two) -> p g two", two=2)
                n2 = MB * NGR * 2
                dve.tensor_tensor(gp[:, 0, 0:n2], pr[:, :, 0], pr[:, :, 1], ALU.max)
                dve.tensor_tensor(gp[:, 1, 0:n2], pr[:, :, 0], pr[:, :, 1], ALU.min)
                dve.drain()
                mx = gp[:, 0, 0:n2].rearrange("p (g two) -> p g two", two=2)
                mn = gp[:, 1, 0:n2].rearrange("p (g two) -> p g two", two=2)
                n1 = MB * NGR
                dve.tensor_tensor(gp[:, 2, 0:n1], mx[:, :, 0], mx[:, :, 1], ALU.max)
                dve.tensor_tensor(gp[:, 3, 0:n1], mx[:, :, 0], mx[:, :, 1], ALU.min)
                dve.tensor_tensor(gp[:, 4, 0:n1], mn[:, :, 0], mn[:, :, 1], ALU.max)
                dve.drain()
                dve.tensor_tensor(gp[:, 5, 0:n1], gp[:, 3, 0:n1], gp[:, 4, 0:n1], ALU.max)
                dve.drain()
                dve.tensor_tensor(gp[:, 6, 0:n1], gp[:, 2, 0:n1], gp[:, 5, 0:n1], ALU.add)
                dve.drain()

                def ranks(dst, val, n, tie):
                    q = "p (m e f) -> p m e f"
                    c1 = cmp1[:, 0:MB * n * n].rearrange(q, m=MB, e=n)
                    c2 = cmp2[:, 0:MB * n * n].rearrange(q, m=MB, e=n)
                    f = val.unsqueeze(2).to_broadcast([P, MB, n, n])
                    e = val.unsqueeze(3).to_broadcast([P, MB, n, n])
                    dve.tensor_tensor(c1, f, e, ALU.is_gt)
                    dve.tensor_tensor(c2, f, e, ALU.is_equal)
                    dve.drain()
                    dve.tensor_tensor(c2, c2, tie.rearrange("p (e f) -> p e f", e=n).unsqueeze(1).to_broadcast(
                        [P, MB, n, n]), ALU.mult)
                    dve.drain()
                    dve.tensor_tensor(c1, c1, c2, ALU.add)
                    dve.drain()
                    dve.tensor_reduce(dst, c1, AX_X, ALU.add)
                    dve.drain()

                gs = gp[:, 6, 0:n1].rearrange("p (m g) -> p m g", m=MB)
                ranks(gp[:, 7, 0:n1].rearrange("p (m g) -> p m g", m=MB), gs, NGR, C["tie4"][:])
                dve.tensor_scalar(gp[:, 5, 0:n1], gp[:, 7, 0:n1], float(GTOP), None, ALU.is_lt)
                dve.drain()
                dve.tensor_scalar(gp[:, 4, 0:n1], gp[:, 5, 0:n1], NEG, -NEG, ALU.mult, ALU.add)
                groups = lambda a: fl(a).rearrange("p (g s) -> p g s", s=GSZ)
                member = lambda a: a.unsqueeze(2).to_broadcast([P, n1, GSZ])
                dve.tensor_tensor(groups(mb[:]), groups(bi[:]), member(gp[:, 5, 0:n1]), ALU.mult)
                dve.drain()
                dve.tensor_tensor(groups(mb[:]), groups(mb[:]), member(gp[:, 4, 0:n1]), ALU.add)
                dve.drain()
                ranks(rank[:], mb[:], NX, C["tie16"][:])
                dve.tensor_scalar(sel[:], rank[:], float(TOPK), None, ALU.is_lt)
                dve.drain()
                for m in range(MB):
                    dve.tensor_tensor(seen[:, m + 1, :], seen[:, m, :], sel[:, m, :], ALU.add).then_inc(chain, 1)
                    dve.wait_ge(chain, b * MB + (m + 1))
                dve.tensor_tensor(ws[:], sc[:], sel[:], ALU.mult).then_inc(sel_ready, 1)
                dve.drain()
                dve.tensor_reduce(tmp4[:, 0:MB], ws[:], AX_X, ALU.add)
                dve.drain()
                dve.tensor_scalar(tmp4[:, 0:MB], tmp4[:, 0:MB], 1e-20, None, ALU.add)
                dve.drain()
                dve.reciprocal(tmp4[:, 0:MB], tmp4[:, 0:MB])
                dve.drain()
                dve.tensor_tensor(ws[:], ws[:], tmp4[:, 0:MB].unsqueeze(2).to_broadcast([P, MB, NX]), ALU.mult)
                dve.drain()
                dve.tensor_scalar(ws[:], ws[:], ROUTE_SCALE, None, ALU.mult)
                oh = oh4[:].rearrange("p (m k e) -> p m k e", m=MB, k=TOPK)
                dve.tensor_tensor(oh, rank[:].unsqueeze(2).to_broadcast([P, MB, TOPK, NX]),
                                  C["iota"][:, 0:TOPK].unsqueeze(1).unsqueeze(3).to_broadcast([P, MB, TOPK, NX]), ALU.is_equal)
                dve.drain()
                dve.tensor_copy(onehot[:, bass.ds(b * MB, MB)].rearrange("p m k e -> p (m k e)"), oh4[:])

                def chosen(dst, val):
                    c1 = cmp1[:, 0:MB * TOPK * NX].rearrange("p (m k e) -> p m k e", m=MB, k=TOPK)
                    dve.tensor_tensor(c1, oh, val, ALU.mult)
                    dve.drain()
                    dve.tensor_reduce(dst, c1, AX_X, ALU.add)
                    dve.drain()

                row = lambda a: a.unsqueeze(2).to_broadcast([P, MB, TOPK, NX])
                chosen(ek[:], row(ws[:]))
                dve.tensor_copy(cw[:, bass.ds(b * MB, MB), :], ek[:])
                dve.drain()
                chosen(ek[:], C["iota"][:, 0:NX].unsqueeze(1).unsqueeze(1).to_broadcast([P, MB, TOPK, NX]))
                dve.wait_ge(pos_ps, b + 1)
                pk = kf[:, 0, :].rearrange("p (m k) -> p m k", m=MB)
                chosen(pk, row(bank[7][:, 0:MB * NX].rearrange("p (m e) -> p m e", m=MB)))
                dve.tensor_copy(seen[:, 0, :], seen[:, MB, :])
                dve.tensor_copy(pos[:, bass.ds(b * MB, MB), :], pk)
                dve.tensor_copy(ki[:, 0, :], kf[:, 0, :])
                dve.drain()
                dve.tensor_scalar(ki[:, 1, :], ki[:, 0, :], P - 1, None, ALU.bitwise_and)
                dve.tensor_scalar(ki[:, 2, :], ki[:, 0, :], P.bit_length() - 1, None, ALU.logical_shift_right)
                dve.drain()
                dve.tensor_copy(kf[:, 0, :], ki[:, 1, :])
                dve.tensor_copy(kf[:, 1, :], ki[:, 2, :])
                dve.drain()
                dve.scalar_tensor_tensor(out=kf[:, 1, :], in0=ek[:].rearrange("p m k -> p (m k)"), scalar=float(JB),
                                         in1=kf[:, 1, :], op0=ALU.mult, op1=ALU.add)
                dve.drain()
                for i in range(MB * TOPK):
                    dve.tensor_scalar(ra[:, i, :], C["iota"][:, 0:P], kf[:, 0, i:i + 1], None, ALU.is_equal)
                    k = dve.tensor_scalar(rb[:, i, :], C["iota"][:], kf[:, 1, i:i + 1], tok4[:, i // TOPK:i // TOPK + 1],
                                          ALU.is_equal, ALU.mult)
                k.then_inc(ab_ready, 1)
                dve.wait_ge(tab_ps, b + 1)
                dve.tensor_tensor(slot_tab[:].rearrange("p h r -> p (h r)"), slot_tab[:].rearrange("p h r -> p (h r)"),
                                  bank[6][:, 0:NCOL], ALU.add)
            dve.drain()
            dve.engine_nop().then_inc(sel_ready, 1)
            dve.wait_ge(count_ps, 1)
            nt, base = d16[:, 0, :], d16[:, 1, :]
            dve.tensor_scalar(nt, bank[7][:, 0:NX], float(P - 1), None, ALU.add)
            dve.drain()
            dve.tensor_copy(d16i[:, 0, :], nt)
            dve.drain()
            dve.tensor_scalar(d16i[:, 1, :], d16i[:, 0, :], P.bit_length() - 1, None, ALU.logical_shift_right)
            dve.drain()
            dve.tensor_copy(nt, d16i[:, 1, :])
            dve.drain()
            big = oh4[:, 0:NX * NX]
            dve.tensor_tensor(big.rearrange("p (e f) -> p e f", e=NX), nt.unsqueeze(1).to_broadcast([P, NX, NX]),
                              C["tie16"][:].rearrange("p (e f) -> p e f", e=NX), ALU.mult)
            dve.drain()
            dve.tensor_reduce(base, big.rearrange("p (e f) -> p e f", e=NX), AX_X, ALU.add)
            dve.drain()
            hot = C["col_onehot"][:].rearrange("p (h e) -> p h e", h=CH)
            for i, v in enumerate((base, nt)):
                o = oh4[:, i * CH * NX:(i + 1) * CH * NX].rearrange("p (h e) -> p h e", h=CH)
                dve.tensor_tensor(o, hot, v.unsqueeze(1).to_broadcast([P, CH, NX]), ALU.mult)
                dve.drain()
                dve.tensor_reduce(d2[:, i, :], o, AX_X, ALU.add)
            dve.drain()
            dve.tensor_tensor(d2[:, 2, :], C["col_piece"][:], d2[:, 1, :], ALU.is_lt)
            dve.tensor_tensor(d2[:, 0, :], d2[:, 0, :], C["col_piece"][:], ALU.add)
            dve.drain()
            dve.scalar_tensor_tensor(out=d2[:, 0, :], in0=d2[:, 0, :], scalar=1.0, in1=d2[:, 2, :], op0=ALU.add, op1=ALU.mult)
            dve.drain()
            dve.tensor_scalar(d2[:, 0, :], d2[:, 0, :], -1.0, None, ALU.add)
            dve.drain()
            for h in range(CH):
                k = dve.tensor_scalar(tile_hot[:, h, :], C["iota"][:, 0:RT], d2[:, 0, h:h + 1], None, ALU.is_equal)
            k.then_inc(tiles_known, 1)

            def ids():
                dve.wait_ge(ids_ps, 1)
                dve.tensor_copy(row_id[:, TB:NT], bank[7][:, 0:RT])
                dve.tensor_copy(expert_id[:, TB:NT], bank[7][:, RT:2 * RT]).then_inc(ids_ready, 1)
                for m in range(TB):
                    o = oh4[:, 0:TOPK * NX].rearrange("p (k e) -> p k e", k=TOPK)
                    dve.tensor_tensor(o, onehot[:, m], base.unsqueeze(1).to_broadcast([P, TOPK, NX]), ALU.mult)
                    dve.drain()
                    dve.tensor_reduce(sl[:, m, :], o, AX_X, ALU.add)
                    dve.drain()
                dve.tensor_scalar(sl[:], sl[:], float(P), float(T), ALU.mult, ALU.add)
                dve.drain()
                dve.tensor_tensor(sl[:], sl[:], pos[:], ALU.add)
                dve.drain()
                dve.tensor_copy(slot_id[:], sl[:]).then_inc(slots_ready, 1)

            def finish_h(t):
                k = t.par
                dve.wait_ge(hT_ps, t.at(1))
                dve.tensor_copy(hT[:, k].rearrange("p c n -> p (c n)"), bank[4][:, 0:FF]).then_inc(hT_sb, 1)
                dve.wait_ge(y_ps, t.at(1))
                if not t.below(2):
                    dve.wait_ge(y_out[k], t.uses(-1) * 16)
                dve.tensor_copy(yy[:, k], bank[5 + k][:]).then_inc(y_sb, 1)

            def step(t):
                k = t.par
                dve.wait_ge(silu_done, t.at(1))
                if not t.below(2):
                    dve.wait_ge(hT_ps, t.at(-1))
                dve.tensor_tensor(hh[:, k], sg[:, k], bank[2 + k][:, FF:2 * FF], ALU.mult).then_inc(h_ready, 1)
                if not t.is_(0):
                    finish_h(t.plus(-1))

            for t in range(3):
                step(Tile(None, t))
            tile_pairs(dve, 3, TB - 3, step)
            ids()
            tile_pairs(dve, TB - 3, NT - 1, step)
            step(Tile(None, NT - 1))
            finish_h(Tile(None, NT - 1))
            with dve.Fori(0, TB // 2) as r:
                for k in range(2):
                    dve.wait_ge(fin_in[k], r * 32 + 32)
                    dve.tensor_tensor(fin[:, k, 0], fin[:, k, 0], fin[:, k, 1], ALU.add)
                    dve.drain()
                    dve.wait_ge(gath_in[k], r * 16 * TOPK + 16 * TOPK)
                    dve.wait_ge(ccw_ready, 2 * r + k + 1)
                    for c in range(TOPK):
                        if c:
                            dve.drain()
                        i = dve.scalar_tensor_tensor(out=fin[:, k, 0], in0=gath[:, k, c], scalar=ccw[:, k, c:c + 1],
                                                     in1=fin[:, k, 0], op0=ALU.mult, op1=ALU.add)
                    i.then_inc(fin_ready, 1)


def kernel(**inputs):
    import concourse.bacc as bacc
    from concourse.bass_utils import run_bass_kernel_spmd

    a = {k.replace("L0_", ""): np.asarray(v) for k, v in inputs.items()}
    put = np.ascontiguousarray
    gate = np.concatenate([a["ffn_shared_gate"][None], a["ffn_gate_proj"]])
    up = np.concatenate([a["ffn_shared_up"][None], a["ffn_up_proj"]])
    down = np.concatenate([a["ffn_shared_down"][None], a["ffn_down_proj"]])
    gu = np.concatenate([gate, up], 1)
    arrays = {
        "x": put(a["attn_x"].reshape(B, MB, P, E).transpose(0, 2, 1, 3)),
        "w_qkv": put(a["attn_w_qkv"].reshape(EC, P, 3 * E).transpose(1, 0, 2)),
        "w_out": put(a["attn_w_out"].reshape(EC, P, E).transpose(1, 0, 2)),
        "ln_scale": put(np.tile(a["attn_ln_scale"], HG)[:, None]),
        "ln_bias": put(np.tile(a["attn_ln_bias"], HG)[:, None]),
        "gate_w": put(a["ffn_gate_weight"].T.reshape(EC, P, NX).transpose(1, 0, 2)),
        "expert_bias": put(np.tile(a["ffn_expert_bias"][None, :], (P, 1))),
        "w_gu": put(gu.transpose(0, 2, 1).reshape(NX + 1, EC, P, 2 * FF).transpose(0, 2, 1, 3)),
        "w_dn": put(down.transpose(0, 2, 1).reshape(NX + 1, FC, P, E).transpose(0, 2, 1, 3).reshape((NX + 1) * P, FC * E)),
    }
    consts = constants()
    nc = bacc.Bacc("TRN2", target_bir_lowering=False, num_devices=1)
    dram = lambda n, v: nc.dram_tensor(n, v.shape, F32, kind="ExternalInput").ap()
    aps = {k: dram(k, v) for k, v in arrays.items()}
    cst = {k: dram("const_" + k, v) for k, v in consts.items()}
    out = nc.dram_tensor("out", (B, N, E), F32, kind="ExternalOutput").ap()
    build(nc, cst=cst, out=out, **aps)
    arrays.update({"const_" + k: v for k, v in consts.items()})
    r = run_bass_kernel_spmd(nc, [arrays], core_ids=[0])
    return r.results[0]["out"]
```

```python
from contextlib import ExitStack

import numpy as np

import concourse.bass as bass
from concourse import mybir

F32 = mybir.dt.float32
F16 = mybir.dt.float16
I32 = mybir.dt.int32
ALU = mybir.AluOpType
ACT = mybir.ActivationFunctionType
AX_X = mybir.AxisListType.X

P = 128
B, N, E = 4, 512, 512
H, D = 16, 32
HG = P // D
NG = H // HG
T = B * N
MB = N // P
EC = E // P
NX, TOPK, NGR, GTOP = 16, 4, 4, 2
GSZ = NX // NGR
FF = 256
FC = FF // P
ROUTE_SCALE = 2.5
EPS = 1e-5
TB = T // P
RT = T * TOPK // P + NX
NT = RT + TB
XS, WS = 1024.0, 256.0
HMAX = 4096.0
NC6 = EC + FC
HC = NC6 // 2
PIECE = HC * E // 2
JB = T // P
NCOL = NX * JB
CH = NCOL // P
NEG = 1.0e30


class Tile:

    def __init__(self, r, lo):
        self.r, self.lo, self.par = r, lo, lo % 2

    def at(self, d=0):
        return self.lo + d if self.r is None else self.r * 2 + (self.lo + d)

    def plus(self, d):
        return Tile(self.r, self.lo + d)

    def uses(self, d=0):
        return self.lo // 2 + 1 + d if self.r is None else self.r + (self.lo // 2 + 1 + d)

    def is_(self, n):
        return self.r is None and self.lo == n

    def below(self, n):
        return self.r is None and self.lo < n

    def shared(self):
        return self.lo >= RT


def tile_pairs(eng, lo, hi, step):
    with eng.Fori(0, (hi - lo) // 2) as r:
        step(Tile(r, lo))
        step(Tile(r, lo + 1))


def constants():
    c = {}
    inv = (1.0 / np.float32(10000.0) ** (np.arange(0, D, 2, dtype=np.float32) / np.float32(D))).astype(np.float32)
    t = np.arange(N, dtype=np.float32)[:, None] * inv[None, :]
    cos, sin = np.cos(t).astype(np.float32), np.sin(t).astype(np.float32)
    lay = lambda a: a.reshape(MB, P, D).transpose(1, 0, 2)
    c["rope_cos"] = lay(np.concatenate([cos, cos], 1))
    c["rope_sin"] = lay(np.concatenate([-sin, sin], 1))
    c["ident"] = np.eye(P)
    c["ident16"] = np.eye(P)
    i = np.arange(P)
    c["causal"] = i[:, None] <= i[None, :]
    c["before"] = i[:, None] < i[None, :]
    e = np.arange(NX)
    c["tie16"] = np.tile((e[None, :] < e[:, None]).reshape(1, NX * NX), (P, 1))
    g = np.arange(NGR)
    c["tie4"] = np.tile((g[None, :] < g[:, None]).reshape(1, NGR * NGR), (P, 1))
    c["iota"] = np.tile(np.arange(NCOL)[None, :], (P, 1))
    col = np.arange(NCOL).reshape(CH, P).T
    c["col_piece"] = col % JB
    c["col_onehot"] = (col // JB)[:, :, None] == e[None, None, :]
    c["col_id"] = np.repeat((col // JB + 1)[:, :, None], P, 2)
    c["token"] = np.arange(T).reshape(TB, P).T
    return {k: np.ascontiguousarray(v.reshape(P, -1).astype(np.float32)) for k, v in c.items()}


def build(nc, x, w_qkv, w_out, ln_scale, ln_bias, gate_w, expert_bias, w_experts, cst, out):
    ctx = ExitStack()
    with ctx:
        sb = lambda n, s, d=F32: ctx.enter_context(nc.sbuf_tensor(n, s, d))
        sem = lambda n: ctx.enter_context(nc.semaphore(n))

        x1_dram = nc.dram_tensor("x1_scratch", [TB, P, E], F32, kind="Internal").ap()
        xn_dram = nc.dram_tensor("xn_scratch", [T, 2 * E], F16, kind="Internal").ap()
        w16_dram = nc.dram_tensor("w16_scratch", [(NX + 1) * P, 2, NC6, E], F16, kind="Internal").ap()
        y_dram = nc.dram_tensor("y_scratch", [RT * P, E], F32, kind="Internal").ap()

        EW = EC * 2 * FF
        arena = sb("arena", [P, (NX + 1) * EW])
        EARLY = 5
        SPLIT = 3
        stage = arena[:, EARLY * EW:EARLY * EW + 2 * HC * E].rearrange("p (j n) -> p j n", j=2)
        halves = arena[:, EARLY * EW + 2 * HC * E:EARLY * EW + 4 * HC * E].bitcast(F16).rearrange(
            "p (j h n) -> p j h n", j=2, h=2)
        top = [(EARLY + SPLIT) * EW]

        def over(shape):
            n = int(np.prod(shape))
            a = arena[:, top[0]:top[0] + n]
            top[0] += n
            assert top[0] <= (NX + 1) * EW
            return a.rearrange("p (a b) -> p a b", a=shape[0]) if len(shape) == 2 else a

        gu = arena[:].bitcast(F16).rearrange("p (e h c n) -> p e h c n", e=NX + 1, h=2, c=EC)
        wqkv = over([EC, 3 * E])
        wout = over([EC, E])
        xnT = over([EC, N])
        qT = over([NG, N])
        kT = over([NG, N])
        s_sq = over([HG, N])
        xres = over([MB, E])
        C = {k: sb("c_" + k, [P, v.shape[1]]) for k, v in cst.items()}
        ident = C["ident"][:]
        ident16 = sb("ident16", [P, P], F16)
        ln_s, ln_b = sb("ln_s", [P, 1]), sb("ln_b", [P, 1])
        eps = sb("eps", [P, 1])
        ones = sb("ones", [P, P])
        gwT = sb("gwT", [P, EC, NX])
        ebias = sb("ebias", [P, NX])
        onehot = sb("onehot", [P, TB, TOPK, NX])
        cw = sb("cw", [P, TB, TOPK])
        pos = sb("pos", [P, TB, TOPK])
        slot_tab = sb("slot_tab", [P, CH, P])
        seen = sb("seen", [P, MB + 1, NX])
        row_id = sb("row_id", [P, RT], I32)
        expert_id = sb("expert_id", [P, RT], I32)
        slot_id = sb("slot_id", [P, TB, TOPK], I32)
        oh4 = sb("oh4", [P, MB * TOPK * NX])
        tmp4 = sb("tmp4", [P, MB])
        tile_hot = sb("tile_hot", [P, CH, RT])
        d16, d16i, d2 = sb("d16", [P, 2, NX]), sb("d16i", [P, 2, NX], I32), sb("d2", [P, 3, CH])
        sl = sb("sl", [P, TB, TOPK])
        att = ExitStack()
        sa = lambda n, s, d=F32: att.enter_context(nc.sbuf_tensor(n, s, d))
        xin = sa("xin", [P, MB, E])
        ra = sa("ra", [P, MB * TOPK, P], F16)
        rb = sa("rb", [P, MB * TOPK, NCOL], F16)
        cmp = rb[:].rearrange("p i n -> p (i n)").bitcast(F32)
        cmp1, cmp2 = cmp[:, 0:MB * NX * NX], cmp[:, MB * NX * NX:2 * MB * NX * NX]
        vtok = sa("vtok", [P, MB, E])
        t1, t2 = s_sq[:, 0:2, :].rearrange("p j n -> p (j n)"), s_sq[:, 2:4, :].rearrange("p j n -> p (j n)")
        qkn = sa("qkn", [P, 2 * E])
        s_p4 = sa("s_p4", [P, 2, HG, N])
        xn2 = s_p4[:, 0]
        x2T = s_p4[:, 1, 0:2, :].rearrange("p j (c n) -> p j c n", c=EC)
        st = sa("st", [P, MB, 6])
        mv = sa("mv", [P, MB, 2])
        sd = sa("sd", [P, MB])
        hs = sa("hs", [P, 3, 2 * H])
        rec = qkn[:, 0:N]
        xn16 = vtok[:].rearrange("p m e -> p (m e)").bitcast(F16).rearrange("p (m h e) -> p m h e", m=MB, h=2)
        attT = xnT
        sc, bi, mb, rank, ws = (sa(n, [P, MB, NX]) for n in ("sc", "bi", "mb", "rank", "ws"))
        sel = sa("sel", [P, MB, NX])
        gp = sa("gp", [P, 8, MB * NGR * 2])
        ek = sa("ek", [P, MB, TOPK])
        ki = sa("ki", [P, 3, MB * TOPK], I32)
        kf = sa("kf", [P, 2, MB * TOPK])
        tok4 = sa("tok4", [P, MB])
        att.close()
        moe = ExitStack()
        sm = lambda n, s, d=F32: moe.enter_context(nc.sbuf_tensor(n, s, d))
        xg = sm("xg", [P, 2, 2 * EC, P], F16)
        gidx = sm("gidx", [P, 2], I32)
        xgT = sm("xgT", [P, 2, 2 * EC, P], F16)
        wd = sm("wd", [P, 2, 2, FC, E], F16)
        sg = sm("sg", [P, 2, FF])
        hh = sm("hh", [P, 2, FF])
        h16 = sm("h16", [P, 2, 2, FF], F16)
        hsc = sm("hsc", [P, 2, 4])
        hT = sm("hT", [P, 2, 2 * FC, P], F16)
        yy = sm("yy", [P, 2, E])
        x1r = sm("x1r", [P, 2, E])
        gath = sm("gath", [P, 2, TOPK, E])
        cidx = sm("cidx", [P, 2, TOPK], I32)
        moe.close()
        print("SBUF LEFT", nc.sbuf_bytes_remaining() if callable(nc.sbuf_bytes_remaining) else nc.sbuf_bytes_remaining, flush=True)

        bank = [ctx.enter_context(nc.psum_tensor(f"bank{i}", [P, 512], F32)) for i in range(8)]
        quad = lambda bk: bk[:].rearrange("p (c n) -> p c n", c=4)
        oct16 = lambda bk: bk[:].bitcast(F16).rearrange("p (c n) -> p c n", c=8)

        consts_in, wqkv_in, wout_in, experts_in = map(sem, ("consts_in", "wqkv_in", "wout_in", "experts_in"))
        stage_in = [sem("stage_in0"), sem("stage_in1")]
        halves_out = [sem("halves_out0"), sem("halves_out1")]
        hi_done, lo_done, xhi_done, xn16_ready, up_used = map(sem, (
            "hi_done", "lo_done", "xhi_done", "xn16_ready", "up_used"))
        xin_in, xres_in, x1_out, xn2_out = map(sem, ("xin_in", "xres_in", "x1_out", "xn2_out"))
        memset_done = sem("memset_done")
        var1, std1, xn_ready = sem("var1"), sem("std1"), sem("xn_ready")
        xT_ps, xT_sb, qkv_ps = sem("xT_ps"), sem("xT_sb"), sem("qkv_ps")
        rope_parts, rotated, mean_ready, centred, squares, hvar, hstd, hrstd, qkn_ready = map(sem, (
            "rope_parts", "rotated", "mean_ready", "centred", "squares", "hvar", "hstd", "hrstd", "qkn_ready"))
        v_sb, qkT_ps, qkT_sb = sem("v_sb"), sem("qkT_ps"), sem("qkT_sb")
        scores_ps, sq_done, p4_done, p4_masked, pv_done, att_done = map(sem, (
            "scores_ps", "sq_done", "p4_done", "p4_masked", "pv_done", "att_done"))
        proj_ps, x1_ready, var2, std2, xn2_ready = map(sem, ("proj_ps", "x1_ready", "var2", "std2", "xn2_ready"))
        x2T_ps, x2T_sb, logits_ps, scores_sig, sel_ready, pos_ps, ab_ready, tab_ps = map(sem, (
            "x2T_ps", "x2T_sb", "logits_ps", "scores_sig", "sel_ready", "pos_ps", "ab_ready", "tab_ps"))
        count_ps, tiles_known, ids_ps, ids_ready, slots_ready = map(sem, (
            "count_ps", "tiles_known", "ids_ps", "ids_ready", "slots_ready"))
        chain = sem("chain")
        xg_in = [sem("xg_in0"), sem("xg_in1")]
        rows_in = [sem("rows_in0"), sem("rows_in1")]
        wd_in = [sem("wd_in0"), sem("wd_in1")]
        y_out = [sem("y_out0"), sem("y_out1")]
        gT_ps, gT_sb, gu_ps, silu_done, h_ready, hT_ps, hT_sb, y_ps, y_sb = map(sem, (
            "gT_ps", "gT_sb", "gu_ps", "silu_done", "h_ready", "hT_ps", "hT_sb", "y_ps", "y_sb"))
        x1r_in = [sem("x1r_in0"), sem("x1r_in1")]
        gath_in = [sem("gath_in0"), sem("gath_in1")]
        fin_out = [sem("fin_out0"), sem("fin_out1")]
        fin_ready = sem("fin_ready")
        NCST = len(cst) + 6

        block = ctx.enter_context(nc.Block())

        def over_tiles(step):
            for t in range(3):
                step(Tile(None, t))
            yield 3, RT - 1
            step(Tile(None, RT - 1))
            step(Tile(None, RT))
            yield RT + 1, NT - 1
            step(Tile(None, NT - 1))

        def all_tiles(eng, step):
            for lo, hi in over_tiles(step):
                tile_pairs(eng, lo, hi, step)

        @block.sync
        def _(sp):
            sp.dma_start(xin[:], x[0]).then_inc(xin_in, 16)
            for k, v in cst.items():
                sp.dma_start(C[k][:], v).then_inc(consts_in, 16)
            for j in range(HG):
                if j < 2:
                    sp.dma_start(ln_s[64 * j:64 * j + 64, :], ln_scale[64 * j:64 * j + 64, :]).then_inc(consts_in, 16)
                else:
                    sp.dma_start(ln_b[64 * j - 128:64 * j - 64, :], ln_bias[64 * j - 128:64 * j - 64, :]).then_inc(consts_in, 16)
            sp.dma_start(gwT[:], gate_w).then_inc(consts_in, 16)
            sp.dma_start(ebias[:], expert_bias).then_inc(consts_in, 16)
            sp.dma_start(wqkv, w_qkv).then_inc(wqkv_in, 16)
            sp.dma_start(xres[:], x[0]).then_inc(xres_in, 16)
            sp.dma_start(wout, w_out).then_inc(wout_in, 16)

            def load_half(n):
                if n >= 2:
                    sp.wait_ge(lo_done, 2 * (n - 1))
                e, j = divmod(n, 2)
                sp.dma_start(stage[:, j], w_experts[e][:, j]).then_inc(stage_in[j], 16)

            def store_half(n):
                sp.wait_ge(lo_done, 2 * (n + 1))
                e, j = divmod(n, 2)
                sp.dma_start(w16_dram[e * P:e * P + P, :, HC * j:HC * j + HC, :].rearrange("p h c n -> p h (c n)"),
                             halves[:, j]).then_inc(halves_out[j], 16)

            def load_experts(lo, hi):
                for j in range(2):
                    sp.wait_ge(halves_out[j], 16 * hi)
                for e in range(lo, hi):
                    sp.dma_start(gu[:, e].rearrange("p h c n -> p h (c n)"),
                                 w16_dram[e * P:e * P + P, :, 0:EC, :].rearrange("p h c n -> p h (c n)")
                                 ).then_inc(experts_in, 16)

            NH = 2 * (NX + 1)
            load_half(0)
            load_half(1)
            for b in range(B):
                sp.wait_ge(xT_ps, MB * (b + 1))
                sp.dma_start(xin[:], x[min(b + 1, B - 1)]).then_inc(xin_in, 16)
                for n in range(8 * b, 8 * b + 8):
                    store_half(n)
                    load_half(n + 2)
                if b == 2:
                    load_experts(0, EARLY)
                sp.wait_ge(x1_ready, MB * (b + 1))
                sp.dma_start(x1_dram[MB * b:MB * b + MB].rearrange("m p e -> p m e"), xres[:]).then_inc(x1_out, 16)
                sp.wait_ge(xn16_ready, b + 1)
                sp.dma_start(xn_dram[N * b:N * b + N].rearrange("(m p) e -> p m e", p=P),
                             xn16.rearrange("p m h e -> p m (h e)")).then_inc(xn2_out, 16)
                if b + 1 < B:
                    sp.wait_ge(x1_out, 16 * (b + 1))
                    sp.dma_start(xres[:], x[b + 1]).then_inc(xres_in, 16)
            for n in range(NH - 2, NH):
                store_half(n)
            sp.wait_ge(proj_ps, MB * B)
            sp.wait_ge(x1_out, 16 * B)
            load_experts(EARLY, NX + 1)
            sp.wait_ge(xn2_out, 16 * B)

            def load_down(t):
                k = t.par
                if not t.below(2):
                    sp.wait_ge(y_ps, t.at(-1))
                e = 0
                if not t.shared():
                    e = sp.value_load(expert_id[0:1, bass.ds(t.at(), 1)], min_val=0, max_val=NX)
                sp.dma_start(wd[:, k].rearrange("p h c n -> p h (c n)"),
                             w16_dram[bass.ds(e * P, P), :, EC:NC6, :].rearrange("p h c n -> p h (c n)")
                             ).then_inc(wd_in[k], 16)

            def load_rows(t):
                k = t.par
                sp.wait_ge(gT_ps, t.at(-1))
                sp.dma_start(xg[:, k].rearrange("p c n -> p (c n)"),
                             xn_dram[bass.ds(t.plus(-RT).at() * P, P), :]).then_inc(rows_in[k], 16)

            def load_residual(s):
                sp.dma_start(x1r[:, s.par], x1_dram[bass.ds(s.at(), 1)].rearrange("m p e -> p (m e)")
                             ).then_inc(x1r_in[s.par], 16)

            def store(t):
                sp.wait_ge(y_sb, t.at(1))
                sp.dma_start(y_dram[bass.ds(t.at() * P, P), :], yy[:, t.par]).then_inc(y_out[t.par], 16)

            def store_result(s):
                sp.wait_ge(fin_ready, s.at(1))
                sp.dma_start(o[bass.ds(s.at(), 1)].rearrange("m p e -> p (m e)"), yy[:, s.par]).then_inc(fin_out[s.par], 16)

            def step(t):
                load_down(t.plus(1))
                if not t.is_(0):
                    store(t.plus(-1))

            def shared_step(t):
                s = t.plus(-RT)
                load_rows(t.plus(2))
                store_result(s.plus(-1))
                load_residual(s.plus(1))

            o = out.rearrange("b (m p) e -> (b m) p e", p=P)
            sp.wait_ge(ids_ready, 1)
            load_down(Tile(None, 0))
            for t in range(3):
                step(Tile(None, t))
            tile_pairs(sp, 3, RT - 1, step)
            load_rows(Tile(None, RT))
            step(Tile(None, RT - 1))
            load_rows(Tile(None, RT + 1))
            load_down(Tile(None, RT + 1))
            store(Tile(None, RT - 1))
            for t in range(2):
                load_residual(Tile(None, t))
            load_rows(Tile(None, RT + 2))
            tile_pairs(sp, RT + 1, NT - 3, shared_step)
            shared_step(Tile(None, NT - 3))
            for t in range(TB - 3, TB):
                store_result(Tile(None, t))
                if t == TB - 3:
                    load_residual(Tile(None, TB - 1))
            for k in range(2):
                sp.wait_ge(fin_out[k], 16 * TB // 2)

        @block.tensor
        def _(pe):
            pe.wait_ge(consts_in, 16 * NCST)
            pe.wait_ge(memset_done, 1)
            def transposed_rows(b, src, ready, m, done, copied):
                pe.wait_ge(ready, b * MB + (m + 1))
                if m >= 2:
                    pe.wait_ge(copied, b * MB + (m - 1))
                for c in range(EC):
                    mm = pe.transpose(quad(bank[4 + m % 2])[:, c], src[:, m, c * P:c * P + P], ident)
                mm.then_inc(done, 1)

            def qkv(b, m):
                pe.wait_ge(xT_sb, b * MB + (m + 1))
                for w in range(3):
                    if m:
                        pe.wait_ge(*((rope_parts, b * MB + m) if w < 2 else (v_sb, b * MB + m)))
                    for c in range(EC):
                        mm = pe.matmul(bank[w][:], xnT[:, c, m * P:m * P + P], wqkv[:, c, w * E:w * E + E],
                                       start=(c == 0), stop=(c == EC - 1))
                    mm.then_inc(qkv_ps, 1)

            def qk_transposes(b, m):
                pe.wait_ge(qkn_ready, b * MB + (m + 1))
                if m:
                    pe.wait_ge(qkT_sb, b * (2 * MB) + 2 * m)
                for w in range(2):
                    for g in range(NG):
                        mm = pe.transpose(quad(bank[6 + w])[:, g], qkn[:, w * E + g * P:w * E + g * P + P], ident)
                    mm.then_inc(qkT_ps, 1)

            def logits(b, m):
                pe.wait_ge(x2T_sb, b * MB + (m + 1))
                for c in range(EC):
                    mm = pe.matmul(bank[3][:, m * NX:m * NX + NX], x2T[:, m % 2, c, :], gwT[:, c, :],
                                   start=(c == 0), stop=(c == EC - 1))
                if m == MB - 1:
                    mm.then_inc(logits_ps, 1)

            def places(b):
                pe.wait_ge(sel_ready, b + 1)
                for m in range(MB):
                    o = bank[4][:, m * NX:m * NX + NX]
                    pe.matmul(o, C["before"][:], sel[:, m, :], start=True, stop=False)
                    mm = pe.matmul(o, ones[:], seen[:, m, :], start=False, stop=True)
                mm.then_inc(pos_ps, 1)

            def table(b):
                pe.wait_ge(ab_ready, b + 1)
                for h in range(CH):
                    for i in range(MB * TOPK):
                        mm = pe.matmul(bank[5][:, h * P:h * P + P], rb[:, i, h * P:h * P + P], ra[:, i, :],
                                       start=(i == 0), stop=(i == MB * TOPK - 1))
                mm.then_inc(tab_ps, 1)

            def sequence(b, before):
                if before is not None:
                    pe.wait_ge(x1_ready, before * MB + 1)
                for m in range(MB):
                    transposed_rows(b, xin, xn_ready, m, xT_ps, xT_sb)
                if before is not None:
                    pe.wait_ge(x1_ready, b * MB)
                pe.wait_ge(wqkv_in, 16)
                for m in range(MB):
                    qkv(b, m)
                    if m:
                        qk_transposes(b, m - 1)
                    if before is not None:
                        if m < 2:
                            pe.wait_ge(xT_sb, b * MB + MB)
                        transposed_rows(before, xn2, xn2_ready, m, x2T_ps, x2T_sb)
                        if m:
                            logits(before, m - 1)
                if before is not None:
                    logits(before, MB - 1)
                qk_transposes(b, MB - 1)
                pe.wait_ge(qkT_sb, b * (2 * MB) + 2 * MB)
                pe.wait_ge(v_sb, b * MB + MB)
                for i in range(NG * MB + 1):
                    if i == 0 and before is not None:
                        pe.wait_ge(scores_sig, b)
                    if i < NG * MB:
                        g, kb = divmod(i, MB)
                        for j in range(HG):
                            if i:
                                pe.wait_ge(sq_done, b * (NG * MB * HG) + (HG * (i - 1) + j + 1))
                            r = slice(D * j, D * j + D)
                            pe.matmul(bank[j][:, 0:N - P * kb], kT[r, g, P * kb:P * kb + P], qT[r, g, P * kb:N],
                                      start=True, stop=True).then_inc(scores_ps, 1)
                    if i:
                        g, kb = divmod(i - 1, MB)
                        if kb == 0 and g:
                            pe.wait_ge(att_done, b * NG + g)
                        for j in range(HG):
                            pe.wait_ge(p4_masked, b * (NG * MB * HG) + (HG * (i - 1) + j + 1))
                            r = slice(D * j, D * j + D)
                            p4 = s_p4[:, (i - 1) % 2, j, 0:N - P * kb]
                            pe.matmul(bank[6][r, P * kb:N], vtok[:, kb, (g * HG + j) * D:(g * HG + j) * D + D], p4,
                                      start=(kb == 0), stop=(kb == MB - 1), skip_group_check=True)
                            mm = pe.matmul(bank[7][r, P * kb:N], ones[:, 0:D], p4,
                                           start=(kb == 0), stop=(kb == MB - 1), skip_group_check=True)
                        mm.then_inc(pv_done, 1)
                    if before is not None:
                        if i == 7:
                            places(before)
                        if i == 15:
                            table(before)
                pe.wait_ge(wout_in, 16)
                pe.wait_ge(att_done, b * NG + NG)
                for m in range(MB):
                    for g in range(NG):
                        mm = pe.matmul(bank[m][:], attT[:, g, m * P:m * P + P], wout[:, g, :],
                                       start=(g == 0), stop=(g == NG - 1))
                    mm.then_inc(proj_ps, 1)

            sequence(0, None)
            with pe.Fori(0, B - 1) as r:
                sequence(r + 1, r)
            for m in range(MB):
                transposed_rows(B - 1, xn2, xn2_ready, m, x2T_ps, x2T_sb)
                if m:
                    logits(B - 1, m - 1)
            logits(B - 1, MB - 1)
            places(B - 1)
            table(B - 1)
            pe.wait_ge(sel_ready, B + 1)
            pe.matmul(bank[7][:, 0:NX], ones[:], seen[:, 0, :], start=True, stop=True).then_inc(count_ps, 1)

            def gather_T(t):
                k = t.par
                if t.shared():
                    pe.wait_ge(rows_in[k], t.plus(-RT).uses() * 16)
                else:
                    pe.wait_ge(xg_in[k], t.uses() * 16)
                if not t.below(2):
                    pe.wait_ge(gT_sb, t.at(-1))
                for c in range(2 * EC):
                    mm = pe.transpose(oct16(bank[k])[:, c], xg[:, k, c], ident16[:])
                mm.then_inc(gT_ps, 1)

            def gate_up(t, e, chunks):
                k = t.par
                for c in chunks:
                    for xh, wh in ((0, 0), (0, 1), (1, 0)):
                        w = gu[:, 0, wh, c, :] if e is None else gu[:, bass.ds(e, 1), wh, c, :]
                        mm = pe.matmul(bank[2 + k][:], xgT[:, k, xh * EC + c, :], w,
                                       start=(c == 0 and xh + wh == 0), stop=(c == EC - 1 and xh == 1))
                return mm

            def hidden_T(t):
                k = t.par
                pe.wait_ge(h_ready, t.at(1))
                if not t.below(1):
                    pe.wait_ge(hT_sb, t.at())
                for c in range(2 * FC):
                    mm = pe.transpose(oct16(bank[4])[:, c], h16[:, k, c // FC, (c % FC) * P:(c % FC) * P + P], ident16[:])
                mm.then_inc(hT_ps, 1)

            def down(t):
                k = t.par
                pe.wait_ge(hT_sb, t.at(1))
                pe.wait_ge(wd_in[k], 16 * (RT // 2 + 1) if t.shared() else t.uses() * 16)
                if not t.below(2):
                    pe.wait_ge(y_sb, t.at(-1))
                for c in range(FC):
                    for hh_, wh in ((0, 0), (0, 1), (1, 0)):
                        mm = pe.matmul(bank[5 + k][:], hT[:, k, hh_ * FC + c, :], wd[:, k, wh, c, :],
                                       start=(c == 0 and hh_ + wh == 0), stop=(c == FC - 1 and hh_ == 1))
                mm.then_inc(y_ps, 1)

            def step(t):
                e = None if t.shared() else pe.value_load(expert_id[0:1, bass.ds(t.at(), 1)], min_val=0, max_val=NX)
                if not t.is_(NT - 1):
                    gather_T(t.plus(1))
                pe.wait_ge(gT_sb, t.at(1))
                if not t.below(2):
                    pe.wait_ge(h_ready, t.at(-1))
                gate_up(t, e, range(EC - 1))
                if not t.is_(0):
                    hidden_T(t.plus(-1))
                gate_up(t, e, range(EC - 1, EC)).then_inc(gu_ps, 1)
                if not t.is_(0):
                    down(t.plus(-1))

            pe.wait_ge(tiles_known, 1)
            for h in range(CH):
                pe.matmul(bank[7][:, 0:RT], slot_tab[:, h, :], tile_hot[:, h, :], start=(h == 0), stop=(h == CH - 1))
            for h in range(CH):
                mm = pe.matmul(bank[7][:, RT:2 * RT], C["col_id"][:, h * P:h * P + P], tile_hot[:, h, :],
                               start=(h == 0), stop=(h == CH - 1))
            mm.then_inc(ids_ps, 1)
            pe.wait_ge(ids_ready, 1)
            pe.wait_ge(experts_in, 16 * (NX + 1))
            gather_T(Tile(None, 0))
            all_tiles(pe, step)
            hidden_T(Tile(None, NT - 1))
            down(Tile(None, NT - 1))

        @block.scalar
        def _(act):
            act.wait_ge(consts_in, 16 * NCST)
            act.wait_ge(memset_done, 1)

            def split_hi(j, q):
                a = slice(q * PIECE, q * PIECE + PIECE)
                act.activation(halves[:, j, 0, a], stage[:, j, a], ACT.Copy, scale=WS).then_inc(hi_done, 1)

            def split_next(b, i):
                j, q = i // 2 % 2, i % 2
                if q == 0:
                    act.wait_ge(stage_in[j], b * (16 * MB) + 16 * (i // 4 + 1))
                    if i >= 4 or not isinstance(b, int):
                        act.wait_ge(halves_out[j], b * (16 * MB) + 16 * (i // 4))
                split_hi(j, q)

            def copy_rows(b, m):
                act.wait_ge(x2T_ps, b * MB + (m + 1))
                act.activation(x2T[:, m % 2], quad(bank[4 + m % 2]), ACT.Copy).then_inc(x2T_sb, 1)

            def gate_scores(b):
                act.wait_ge(logits_ps, b + 1)
                act.activation(sc[:].rearrange("p m e -> p (m e)"), bank[3][:, 0:MB * NX], ACT.Sigmoid).then_inc(scores_sig, 1)

            def qkT(b, m):
                for w, dst in enumerate((qT, kT)):
                    act.wait_ge(qkT_ps, b * (2 * MB) + (2 * m + w + 1))
                    act.activation(dst[:, :, m * P:m * P + P], quad(bank[6 + w]), ACT.Identity,
                                   bias=ln_b[:, 0:1], scale=ln_s[:, 0:1]).then_inc(qkT_sb, 1)

            def deviation(n):
                act.wait_ge(var1, n)
                act.activation(sd[:], mv[:, :, 1], ACT.Sqrt, bias=eps[:, 0:1]).then_inc(std1, 1)

            def sequence(b, before):
                for m in range(MB):
                    act.wait_ge(xT_ps, b * MB + (m + 1))
                    act.activation(xnT[:, :, m * P:m * P + P], quad(bank[4 + m % 2]), ACT.Copy).then_inc(xT_sb, 1)
                for m in range(MB):
                    act.wait_ge(qkv_ps, b * (3 * MB) + (3 * m + 3))
                    if m == 0 and before is not None:
                        act.wait_ge(xn2_out, b * 16)
                    act.activation(vtok[:, m, :], bank[2][:], ACT.Copy).then_inc(v_sb, 1)
                    act.wait_ge(centred, b * MB + (m + 1))
                    act.activation(t2[:], t1[:], ACT.Square).then_inc(squares, 1)
                    act.wait_ge(hvar, b * MB + (m + 1))
                    act.activation(hs[:, 1, :], hs[:, 0, :], ACT.Sqrt, bias=eps[:, 0:1], scale=1.0 / D).then_inc(hstd, 1)
                    if m:
                        qkT(b, m - 1)
                    if before is not None:
                        copy_rows(before, m)
                if before is not None:
                    gate_scores(before)
                qkT(b, MB - 1)
                for i in range(NG * MB):
                    kb = i % MB
                    for j in range(HG):
                        n = HG * i + j
                        act.wait_ge(scores_ps, b * (NG * MB * HG) + (n + 1))
                        if i:
                            act.wait_ge(p4_done, b * (NG * MB * HG) + (n - HG + 1))
                        act.activation(s_sq[:, j, 0:N - P * kb], bank[j][:, 0:N - P * kb], ACT.Square).then_inc(sq_done, 1)
                    split_next(b, i)
                    if i == 13:
                        deviation(b + 2)
                act.wait_ge(var2, b + 1)
                act.activation(sd[:], mv[:, :, 1], ACT.Sqrt, bias=eps[:, 0:1]).then_inc(std2, 1)
                for m in range(MB):
                    act.wait_ge(xn2_ready, b * MB + (m + 1))
                    act.activation(xn16[:, m, 0, :], xn2[:, m, :], ACT.Copy, scale=XS).then_inc(xhi_done, 1)

            deviation(1)
            sequence(0, None)
            with act.Fori(0, B - 1) as r:
                sequence(r + 1, r)
            for m in range(MB):
                copy_rows(B - 1, m)
            gate_scores(B - 1)
            for i in range(4):
                split_next(B, i)

            def copy_hidden(t):
                k = t.par
                act.wait_ge(hT_ps, t.at(1))
                if not t.below(2):
                    act.wait_ge(y_ps, t.at(-1))
                act.activation(hT[:, k], oct16(bank[4])[:, 0:2 * FC], ACT.Copy).then_inc(hT_sb, 1)

            def copy_T(t):
                k = t.par
                act.wait_ge(gT_ps, t.at(1))
                if not t.below(2):
                    act.wait_ge(gu_ps, t.at(-1))
                act.activation(xgT[:, k], oct16(bank[k]), ACT.Copy).then_inc(gT_sb, 1)

            def step(t):
                k = t.par
                if not t.is_(NT - 1):
                    copy_T(t.plus(1))
                if not t.is_(0):
                    copy_hidden(t.plus(-1))
                act.wait_ge(gu_ps, t.at(1))
                if not t.below(2):
                    act.wait_ge(up_used, t.at(-1))
                act.activation(sg[:, k], bank[2 + k][:, 0:FF], ACT.Silu, scale=1.0 / (XS * WS)).then_inc(silu_done, 1)

            act.wait_ge(ab_ready, B)
            copy_T(Tile(None, 0))
            all_tiles(act, step)
            copy_hidden(Tile(None, NT - 1))

        @block.gpsimd
        def _(pool):
            pool.memset(ones[:], 1.0)
            pool.memset(seen[:, 0, :], 0.0)
            pool.memset(slot_tab[:], 0.0)
            pool.memset(eps[:], EPS)
            pool.drain()
            pool.memset(tile_hot[:], 0.0).then_inc(memset_done, 1)
            pool.wait_ge(consts_in, 16 * NCST)
            heads = lambda a: a.rearrange("p (h d) -> p h d", d=D)
            per_head = lambda a: a.unsqueeze(2).to_broadcast([P, 2 * H, D])
            def sequence(b):
                for m in range(MB):
                    pool.wait_ge(rope_parts, b * MB + (m + 1))
                    pool.tensor_tensor(t1[:], t1[:], t2[:], ALU.add).then_inc(rotated, 1)
                    pool.wait_ge(mean_ready, b * MB + (m + 1))
                    pool.tensor_tensor(heads(t1), heads(t1), per_head(hs[:, 0, :]), ALU.subtract).then_inc(centred, 1)
                    pool.wait_ge(hrstd, b * MB + (m + 1))
                    if m:
                        pool.wait_ge(qkT_ps, b * (2 * MB) + 2 * m)
                    pool.tensor_tensor(heads(qkn[:]), heads(t1), per_head(hs[:, 2, :]), ALU.mult).then_inc(qkn_ready, 1)
                for n in range(NG * MB * HG):
                    pool.wait_ge(p4_done, b * (NG * MB * HG) + (n + 1))
                    d = s_p4[:, (n // HG) % 2, n % HG, 0:P]
                    pool.tensor_tensor(d, d, C["causal"][:], ALU.mult).then_inc(p4_masked, 1)
            sequence(0)
            with pool.Fori(0, B - 1) as r:
                sequence(r + 1)

            def step(t):
                k = t.par
                if not t.below(2):
                    pool.wait_ge(gT_ps, t.at(-1))
                pool.tensor_copy(gidx[:, k:k + 1], row_id[:, bass.ds(t.at(), 1)])
                pool.drain()
                pool.indirect_dma_start(out=xg[:, k].rearrange("p c n -> p (c n)"), out_offset=None, in_=xn_dram,
                                        in_offset=bass.IndirectOffsetOnAxis(ap=gidx[:, k:k + 1], axis=0)
                                        ).then_inc(xg_in[k], 16)
            pool.wait_ge(ab_ready, B)
            pool.wait_ge(xn2_out, 16 * B)
            pool.wait_ge(x1_out, 16 * B)
            pool.wait_ge(tab_ps, B)
            pool.wait_ge(ids_ready, 1)
            for t in range(4):
                step(Tile(None, t))
            tile_pairs(pool, 4, RT, step)

            def gather_slots(t):
                k = t.par
                if not (t.is_(0) or t.is_(1)):
                    pool.wait_ge(fin_ready, t.at(-1))
                pool.tensor_copy(cidx[:, k], slot_id[:, bass.ds(t.at(), 1), :].rearrange("p a k -> p (a k)"))
                pool.drain()
                for c in range(TOPK):
                    pool.indirect_dma_start(out=gath[:, k, c], out_offset=None, in_=y_dram,
                                            in_offset=bass.IndirectOffsetOnAxis(ap=cidx[:, k, c:c + 1], axis=0)
                                            ).then_inc(gath_in[k], 16)
            pool.wait_ge(slots_ready, 1)
            for k in range(2):
                pool.wait_ge(y_out[k], 16 * RT // 2)
            for t in range(2):
                gather_slots(Tile(None, t))
            tile_pairs(pool, 2, TB, gather_slots)

        @block.vector
        def _(dve):
            dve.wait_ge(consts_in, 16 * NCST)
            dve.wait_ge(memset_done, 1)
            heads = lambda a: a.rearrange("p (h d) -> p h d", d=D)

            def norm_stats(m, src, last):
                dve.bn_stats(st[:, m, :], src[:, m, :])
                if last is not None:
                    dve.drain()
                    for k in range(MB):
                        i = dve.bn_aggr(mv[:, k, :], st[:, k, :])
                    i.then_inc(last, 1)

            def normed(dst, src, ready):
                dve.reciprocal(sd[:], sd[:])
                dve.drain()
                for m in range(MB):
                    dve.tensor_scalar(dst[:, m, :], src[:, m, :], mv[:, m, 0:1], sd[:, m:m + 1],
                                      ALU.subtract, ALU.mult).then_inc(ready, 1)

            def split_lo(j, q):
                a = slice(q * PIECE, q * PIECE + PIECE)
                dve.scalar_tensor_tensor(out=halves[:, j, 1, a], in0=stage[:, j, a], scalar=WS, in1=halves[:, j, 0, a],
                                         op0=ALU.mult, op1=ALU.subtract).then_inc(lo_done, 1)

            dve.tensor_copy(ident16[:], C["ident16"][:]).then_inc(chain, 1)
            fl = lambda a: a.rearrange("p m e -> p (m e)")
            n1, n2 = MB * NGR, MB * NGR * 2
            oh = oh4[:].rearrange("p (m k e) -> p m k e", m=MB, k=TOPK)
            row = lambda a: a.unsqueeze(2).to_broadcast([P, MB, TOPK, NX])
            member = lambda a: a.unsqueeze(2).to_broadcast([P, n1, GSZ])
            groups = lambda a: fl(a).rearrange("p (g s) -> p g s", s=GSZ)

            def compare(val, n):
                q = "p (m e f) -> p m e f"
                c1 = cmp1[:, 0:MB * n * n].rearrange(q, m=MB, e=n)
                c2 = cmp2[:, 0:MB * n * n].rearrange(q, m=MB, e=n)
                f = val.unsqueeze(2).to_broadcast([P, MB, n, n])
                e = val.unsqueeze(3).to_broadcast([P, MB, n, n])
                dve.tensor_tensor(c1, f, e, ALU.is_gt)
                dve.tensor_tensor(c2, f, e, ALU.is_equal)
                dve.drain()

            def ranks(dst, n, tie):
                q = "p (m e f) -> p m e f"
                c1 = cmp1[:, 0:MB * n * n].rearrange(q, m=MB, e=n)
                c2 = cmp2[:, 0:MB * n * n].rearrange(q, m=MB, e=n)
                dve.tensor_tensor(c2, c2, tie.rearrange("p (e f) -> p e f", e=n).unsqueeze(1).to_broadcast(
                    [P, MB, n, n]), ALU.mult)
                dve.drain()
                dve.tensor_tensor(c1, c1, c2, ALU.add)
                dve.drain()
                dve.tensor_reduce(dst, c1, AX_X, ALU.add)
                dve.drain()

            def group_sums(b):
                dve.tensor_copy(tok4[:], C["token"][:, bass.ds(b * MB, MB)])
                dve.wait_ge(scores_sig, b + 1)
                dve.tensor_tensor(bi[:], sc[:], ebias[:].unsqueeze(1).to_broadcast([P, MB, NX]), ALU.add)
                dve.drain()
                pr = fl(bi[:]).rearrange("p (g two) -> p g two", two=2)
                dve.tensor_tensor(gp[:, 0, 0:n2], pr[:, :, 0], pr[:, :, 1], ALU.max)
                dve.tensor_tensor(gp[:, 1, 0:n2], pr[:, :, 0], pr[:, :, 1], ALU.min)
                dve.drain()
                mx = gp[:, 0, 0:n2].rearrange("p (g two) -> p g two", two=2)
                mn = gp[:, 1, 0:n2].rearrange("p (g two) -> p g two", two=2)
                dve.tensor_tensor(gp[:, 2, 0:n1], mx[:, :, 0], mx[:, :, 1], ALU.max)
                dve.tensor_tensor(gp[:, 3, 0:n1], mx[:, :, 0], mx[:, :, 1], ALU.min)
                dve.tensor_tensor(gp[:, 4, 0:n1], mn[:, :, 0], mn[:, :, 1], ALU.max)
                dve.drain()
                dve.tensor_tensor(gp[:, 5, 0:n1], gp[:, 3, 0:n1], gp[:, 4, 0:n1], ALU.max)
                dve.drain()
                dve.tensor_tensor(gp[:, 6, 0:n1], gp[:, 2, 0:n1], gp[:, 5, 0:n1], ALU.add)
                dve.drain()


            def group_choice():
                gs = gp[:, 6, 0:n1].rearrange("p (m g) -> p m g", m=MB)
                compare(gs, NGR)
                ranks(gp[:, 7, 0:n1].rearrange("p (m g) -> p m g", m=MB), NGR, C["tie4"][:])
                dve.tensor_scalar(gp[:, 5, 0:n1], gp[:, 7, 0:n1], float(GTOP), None, ALU.is_lt)
                dve.drain()
                dve.tensor_scalar(gp[:, 4, 0:n1], gp[:, 5, 0:n1], NEG, -NEG, ALU.mult, ALU.add)
                dve.tensor_tensor(groups(mb[:]), groups(bi[:]), member(gp[:, 5, 0:n1]), ALU.mult)
                dve.drain()
                dve.tensor_tensor(groups(mb[:]), groups(mb[:]), member(gp[:, 4, 0:n1]), ALU.add)
                dve.drain()

            def expert_choice():
                ranks(rank[:], NX, C["tie16"][:])
                dve.tensor_scalar(sel[:], rank[:], float(TOPK), None, ALU.is_lt)
                dve.drain()
                for m in range(MB):
                    i = dve.tensor_tensor(seen[:, m + 1, :], seen[:, m, :], sel[:, m, :], ALU.add)
                    if m == MB - 1:
                        i.then_inc(sel_ready, 1)
                    dve.drain()

            def choice_weights():
                dve.tensor_tensor(ws[:], sc[:], sel[:], ALU.mult)
                dve.drain()
                dve.tensor_reduce(tmp4[:, 0:MB], ws[:], AX_X, ALU.add)
                dve.drain()
                dve.tensor_scalar(tmp4[:, 0:MB], tmp4[:, 0:MB], 1e-20, None, ALU.add)
                dve.drain()
                dve.reciprocal(tmp4[:, 0:MB], tmp4[:, 0:MB])
                dve.drain()
                dve.tensor_tensor(ws[:], ws[:], tmp4[:, 0:MB].unsqueeze(2).to_broadcast([P, MB, NX]), ALU.mult)
                dve.drain()
                dve.tensor_scalar(ws[:], ws[:], ROUTE_SCALE, None, ALU.mult)
                oh = oh4[:].rearrange("p (m k e) -> p m k e", m=MB, k=TOPK)
                dve.tensor_tensor(oh, rank[:].unsqueeze(2).to_broadcast([P, MB, TOPK, NX]),
                                  C["iota"][:, 0:TOPK].unsqueeze(1).unsqueeze(3).to_broadcast([P, MB, TOPK, NX]), ALU.is_equal)
                dve.drain()


            def chosen(dst, val):
                c1 = cmp1[:, 0:MB * TOPK * NX].rearrange("p (m k e) -> p m k e", m=MB, k=TOPK)
                dve.tensor_tensor(c1, oh, val, ALU.mult)
                dve.drain()
                dve.tensor_reduce(dst, c1, AX_X, ALU.add)
                dve.drain()


            def choice_values(b):
                dve.tensor_copy(onehot[:, bass.ds(b * MB, MB)].rearrange("p m k e -> p (m k e)"), oh4[:])
                chosen(ek[:], row(ws[:]))
                dve.tensor_copy(cw[:, bass.ds(b * MB, MB), :], ek[:])
                dve.drain()
                chosen(ek[:], C["iota"][:, 0:NX].unsqueeze(1).unsqueeze(1).to_broadcast([P, MB, TOPK, NX]))

            def choice_places(b):
                dve.wait_ge(pos_ps, b + 1)
                pk = kf[:, 0, :].rearrange("p (m k) -> p m k", m=MB)
                chosen(pk, row(bank[4][:, 0:MB * NX].rearrange("p (m e) -> p m e", m=MB)))
                dve.tensor_copy(seen[:, 0, :], seen[:, MB, :])
                dve.tensor_copy(pos[:, bass.ds(b * MB, MB), :], pk)
                dve.tensor_copy(ki[:, 0, :], kf[:, 0, :])
                dve.drain()
                dve.tensor_scalar(ki[:, 1, :], ki[:, 0, :], P - 1, None, ALU.bitwise_and)
                dve.tensor_scalar(ki[:, 2, :], ki[:, 0, :], P.bit_length() - 1, None, ALU.logical_shift_right)
                dve.drain()
                dve.tensor_copy(kf[:, 0, :], ki[:, 1, :])
                dve.tensor_copy(kf[:, 1, :], ki[:, 2, :])
                dve.drain()
                dve.scalar_tensor_tensor(out=kf[:, 1, :], in0=ek[:].rearrange("p m k -> p (m k)"), scalar=float(JB),
                                         in1=kf[:, 1, :], op0=ALU.mult, op1=ALU.add)
                dve.drain()

            def place_rows(m):
                for i in range(m * TOPK, m * TOPK + TOPK):
                    dve.tensor_scalar(ra[:, i, :], C["iota"][:, 0:P], kf[:, 0, i:i + 1], None, ALU.is_equal)
                    k = dve.tensor_scalar(rb[:, i, :], C["iota"][:], kf[:, 1, i:i + 1], tok4[:, i // TOPK:i // TOPK + 1],
                                          ALU.is_equal, ALU.mult)
                if m == MB - 1:
                    k.then_inc(ab_ready, 1)

            def add_table(b):
                dve.wait_ge(tab_ps, b + 1)
                dve.tensor_tensor(slot_tab[:].rearrange("p h r -> p (h r)"), slot_tab[:].rearrange("p h r -> p (h r)"),
                                  bank[5][:, 0:NCOL], ALU.add)

            def first_norm_stats(n):
                dve.wait_ge(xin_in, n * 16)
                for m in range(MB):
                    norm_stats(m, xin, var1 if m == MB - 1 else None)

            def first_norm(n):
                dve.wait_ge(std1, n)
                normed(xin, xin, xn_ready)

            def finish(b, g):
                dve.wait_ge(pv_done, b * (NG * MB) + (g * MB + MB))
                dve.reciprocal(rec, bank[7][:])
                dve.drain()
                dve.tensor_tensor(attT[:, g, :], bank[6][:], rec, ALU.mult).then_inc(att_done, 1)

            def sequence(b, before):
                for m in range(MB):
                    dve.wait_ge(qkv_ps, b * (3 * MB) + (3 * m + 2))
                    if m:
                        dve.wait_ge(qkn_ready, b * MB + m)
                    cos = C["rope_cos"][:, m * D:m * D + D].unsqueeze(1).to_broadcast([P, H, D])
                    for w in range(2):
                        ps, a1, a2 = heads(bank[w][:]), heads(t1[:, w * E:w * E + E]), heads(t2[:, w * E:w * E + E])
                        dve.tensor_tensor(a1, ps, cos, ALU.mult)
                        for h in range(2):
                            lo, hi = h * D // 2, (1 - h) * D // 2
                            sin = C["rope_sin"][:, m * D + lo:m * D + lo + D // 2].unsqueeze(1).to_broadcast([P, H, D // 2])
                            i = dve.tensor_tensor(a2[:, :, lo:lo + D // 2], ps[:, :, hi:hi + D // 2], sin, ALU.mult)
                    i.then_inc(rope_parts, 1)
                    dve.wait_ge(rotated, b * MB + (m + 1))
                    dve.tensor_reduce(hs[:, 0, :], heads(t1), AX_X, ALU.add)
                    dve.drain()
                    dve.tensor_scalar(hs[:, 0, :], hs[:, 0, :], 1.0 / D, None, ALU.mult).then_inc(mean_ready, 1)
                    dve.wait_ge(squares, b * MB + (m + 1))
                    dve.tensor_reduce(hs[:, 0, :], heads(t2), AX_X, ALU.add).then_inc(hvar, 1)
                    dve.wait_ge(hstd, b * MB + (m + 1))
                    dve.reciprocal(hs[:, 2, :], hs[:, 1, :]).then_inc(hrstd, 1)

                for i in range(NG * MB):
                    kb = i % MB
                    if i >= 2:
                        dve.wait_ge(pv_done, b * (NG * MB) + (i - 1))
                    for j in range(HG):
                        dve.wait_ge(sq_done, b * (NG * MB * HG) + (HG * i + j + 1))
                        s2 = s_sq[:, j, 0:N - P * kb]
                        dve.tensor_tensor(s_p4[:, i % 2, j, 0:N - P * kb], s2, s2, ALU.mult).then_inc(p4_done, 1)
                    if i and kb == 0:
                        finish(b, i // MB - 1)
                    dve.wait_ge(hi_done, b * (NG * MB) + (i + 1))
                    split_lo(i // 2 % 2, i % 2)
                    if before is not None:
                        if i == 0:
                            group_sums(before)
                        elif i == 1:
                            group_choice()
                        elif i == 2:
                            compare(mb[:], NX)
                        elif i == 3:
                            expert_choice()
                        elif i == 5:
                            choice_weights()
                        elif i == 6:
                            choice_values(before)
                        elif i == 8:
                            choice_places(before)
                        elif 9 <= i < 9 + MB:
                            place_rows(i - 9)
                    if i == 12:
                        first_norm_stats(b + 2)
                    if i == 14:
                        first_norm(b + 2)
                finish(b, NG - 1)
                if before is not None:
                    add_table(before)
                dve.wait_ge(xres_in, b * 16 + 16)
                for m in range(MB):
                    dve.wait_ge(proj_ps, b * MB + (m + 1))
                    dve.tensor_tensor(xres[:, m, :], xres[:, m, :], bank[m][:], ALU.add).then_inc(x1_ready, 1)
                dve.drain()
                for m in range(MB):
                    norm_stats(m, xres, var2 if m == MB - 1 else None)
                dve.wait_ge(std2, b + 1)
                normed(xn2, xres, xn2_ready)
                for m in range(MB):
                    dve.wait_ge(xhi_done, b * MB + (m + 1))
                    i = dve.scalar_tensor_tensor(out=xn16[:, m, 1, :], in0=xn2[:, m, :], scalar=XS, in1=xn16[:, m, 0, :],
                                                 op0=ALU.mult, op1=ALU.subtract)
                i.then_inc(xn16_ready, 1)

            first_norm_stats(1)
            first_norm(1)
            sequence(0, None)
            with dve.Fori(0, B - 1) as r:
                sequence(r + 1, r)
            b = B - 1
            group_sums(b)
            group_choice()
            compare(mb[:], NX)
            expert_choice()
            choice_weights()
            choice_values(b)
            choice_places(b)
            for m in range(MB):
                place_rows(m)
            add_table(b)
            for i in range(4):
                dve.wait_ge(hi_done, NG * MB * B + i + 1)
                split_lo(i // 2, i % 2)
            dve.drain()
            dve.engine_nop().then_inc(sel_ready, 1)
            dve.wait_ge(count_ps, 1)
            nt, base = d16[:, 0, :], d16[:, 1, :]
            dve.tensor_scalar(nt, bank[7][:, 0:NX], float(P - 1), None, ALU.add)
            dve.drain()
            dve.tensor_copy(d16i[:, 0, :], nt)
            dve.drain()
            dve.tensor_scalar(d16i[:, 1, :], d16i[:, 0, :], P.bit_length() - 1, None, ALU.logical_shift_right)
            dve.drain()
            dve.tensor_copy(nt, d16i[:, 1, :])
            dve.drain()
            big = oh4[:, 0:NX * NX]
            dve.tensor_tensor(big.rearrange("p (e f) -> p e f", e=NX), nt.unsqueeze(1).to_broadcast([P, NX, NX]),
                              C["tie16"][:].rearrange("p (e f) -> p e f", e=NX), ALU.mult)
            dve.drain()
            dve.tensor_reduce(base, big.rearrange("p (e f) -> p e f", e=NX), AX_X, ALU.add)
            dve.drain()
            hot = C["col_onehot"][:].rearrange("p (h e) -> p h e", h=CH)
            for i, v in enumerate((base, nt)):
                o = oh4[:, i * CH * NX:(i + 1) * CH * NX].rearrange("p (h e) -> p h e", h=CH)
                dve.tensor_tensor(o, hot, v.unsqueeze(1).to_broadcast([P, CH, NX]), ALU.mult)
                dve.drain()
                dve.tensor_reduce(d2[:, i, :], o, AX_X, ALU.add)
            dve.drain()
            dve.tensor_tensor(d2[:, 2, :], C["col_piece"][:], d2[:, 1, :], ALU.is_lt)
            dve.tensor_tensor(d2[:, 0, :], d2[:, 0, :], C["col_piece"][:], ALU.add)
            dve.drain()
            dve.scalar_tensor_tensor(out=d2[:, 0, :], in0=d2[:, 0, :], scalar=1.0, in1=d2[:, 2, :], op0=ALU.add, op1=ALU.mult)
            dve.drain()
            dve.tensor_scalar(d2[:, 0, :], d2[:, 0, :], -1.0, None, ALU.add)
            dve.drain()
            for h in range(CH):
                k = dve.tensor_scalar(tile_hot[:, h, :], C["iota"][:, 0:RT], d2[:, 0, h:h + 1], None, ALU.is_equal)
            k.then_inc(tiles_known, 1)

            dve.wait_ge(ids_ps, 1)
            dve.tensor_copy(row_id[:], bank[7][:, 0:RT])
            dve.tensor_copy(expert_id[:], bank[7][:, RT:2 * RT]).then_inc(ids_ready, 1)
            for m in range(0, TB, MB):
                o = oh4[:].rearrange("p (m k e) -> p m k e", m=MB, k=TOPK)
                dve.tensor_tensor(o, onehot[:, m:m + MB], base.unsqueeze(1).unsqueeze(1).to_broadcast(
                    [P, MB, TOPK, NX]), ALU.mult)
                dve.drain()
                dve.tensor_reduce(sl[:, m:m + MB, :], o, AX_X, ALU.add)
                dve.drain()
            dve.scalar_tensor_tensor(out=sl[:], in0=sl[:], scalar=float(P), in1=pos[:], op0=ALU.mult, op1=ALU.add)
            dve.drain()
            dve.tensor_copy(slot_id[:], sl[:]).then_inc(slots_ready, 1)

            def hidden(t):
                k = t.par
                h, mx = hh[:, k], hsc[:, k, 0:1]
                dve.wait_ge(silu_done, t.at(1))
                dve.tensor_tensor(h, sg[:, k], bank[2 + k][:, FF:2 * FF], ALU.mult).then_inc(up_used, 1)
                dve.drain()
                dve.tensor_reduce(mx, h, AX_X, ALU.max, apply_absolute_value=True)
                dve.drain()
                dve.tensor_scalar(hsc[:, k, 1:2], mx, 1e-30, 1.0 / HMAX, ALU.max, ALU.mult)
                dve.drain()
                dve.reciprocal(hsc[:, k, 2:3], hsc[:, k, 1:2])
                dve.tensor_scalar(hsc[:, k, 3:4], hsc[:, k, 1:2], 1.0 / (XS * WS * WS), None, ALU.mult)
                dve.drain()
                if not t.below(2):
                    dve.wait_ge(hT_ps, t.at(-1))
                dve.tensor_scalar(h16[:, k, 0], h, hsc[:, k, 2:3], None, ALU.mult)
                dve.drain()
                dve.scalar_tensor_tensor(out=h16[:, k, 1], in0=h, scalar=hsc[:, k, 2:3], in1=h16[:, k, 0],
                                         op0=ALU.mult, op1=ALU.subtract).then_inc(h_ready, 1)

            def output(t):
                k = t.par
                if t.shared():
                    s = t.plus(-RT)
                    dve.wait_ge(x1r_in[k], s.uses() * 16)
                    if s.is_(0) or s.is_(1):
                        dve.wait_ge(y_out[k], 16 * RT // 2)
                    else:
                        dve.wait_ge(fin_out[k], s.uses(-1) * 16)
                    dve.wait_ge(y_ps, t.at(1))
                    dve.scalar_tensor_tensor(out=yy[:, k], in0=bank[5 + k][:], scalar=hsc[:, k, 3:4], in1=x1r[:, k],
                                             op0=ALU.mult, op1=ALU.add).then_inc(y_sb, 1)
                    dve.drain()
                    dve.wait_ge(gath_in[k], s.uses() * (16 * TOPK))
                    for c in range(TOPK):
                        if c:
                            dve.drain()
                        i = dve.scalar_tensor_tensor(out=yy[:, k], in0=gath[:, k, c], in1=yy[:, k],
                                                     scalar=cw[:, bass.ds(s.at(), 1), c:c + 1].rearrange("p a k -> p (a k)"),
                                                     op0=ALU.mult, op1=ALU.add)
                    i.then_inc(fin_ready, 1)
                    return
                if not t.below(2):
                    dve.wait_ge(y_out[k], t.uses(-1) * 16)
                dve.wait_ge(y_ps, t.at(1))
                dve.tensor_scalar(yy[:, k], bank[5 + k][:], hsc[:, k, 3:4], None, ALU.mult).then_inc(y_sb, 1)

            def step(t):
                hidden(t)
                if not t.is_(0):
                    output(t.plus(-1))

            all_tiles(dve, step)
            output(Tile(None, NT - 1))


def kernel(**inputs):
    import concourse.bacc as bacc
    from concourse.bass_utils import run_bass_kernel_spmd

    a = {k.replace("L0_", ""): np.asarray(v) for k, v in inputs.items()}
    put = np.ascontiguousarray
    gate = np.concatenate([a["ffn_shared_gate"][None], a["ffn_gate_proj"]])
    up = np.concatenate([a["ffn_shared_up"][None], a["ffn_up_proj"]])
    down = np.concatenate([a["ffn_shared_down"][None], a["ffn_down_proj"]])
    gu = np.concatenate([gate, up], 1).transpose(0, 2, 1).reshape(NX + 1, EC, P, 2 * FF)
    dn = down.transpose(0, 2, 1).reshape(NX + 1, FC, P, E)
    chunks = np.concatenate([gu, dn], 1).transpose(0, 2, 1, 3)
    arrays = {
        "x": put(a["attn_x"].reshape(B, MB, P, E).transpose(0, 2, 1, 3)),
        "w_qkv": put(a["attn_w_qkv"].reshape(EC, P, 3 * E).transpose(1, 0, 2)),
        "w_out": put(a["attn_w_out"].reshape(EC, P, E).transpose(1, 0, 2)),
        "ln_scale": put(np.tile(a["attn_ln_scale"], HG)[:, None]),
        "ln_bias": put(np.tile(a["attn_ln_bias"], HG)[:, None]),
        "gate_w": put(a["ffn_gate_weight"].T.reshape(EC, P, NX).transpose(1, 0, 2)),
        "expert_bias": put(np.tile(a["ffn_expert_bias"][None, :], (P, 1))),
        "w_experts": put(chunks.reshape(NX + 1, P, 2, HC * E)),
    }
    consts = constants()
    nc = bacc.Bacc("TRN2", target_bir_lowering=False, num_devices=1)
    dram = lambda n, v: nc.dram_tensor(n, v.shape, F32, kind="ExternalInput").ap()
    aps = {k: dram(k, v) for k, v in arrays.items()}
    cst = {k: dram("const_" + k, v) for k, v in consts.items()}
    out = nc.dram_tensor("out", (B, N, E), F32, kind="ExternalOutput").ap()
    build(nc, cst=cst, out=out, **aps)
    arrays.update({"const_" + k: v for k, v in consts.items()})
    r = run_bass_kernel_spmd(nc, [arrays], core_ids=[0])
    return r.results[0]["out"]
```

```python
from contextlib import ExitStack

import numpy as np

import concourse.bass as bass
from concourse import mybir

F32 = mybir.dt.float32
F16 = mybir.dt.float16
I32 = mybir.dt.int32
ALU = mybir.AluOpType
ACT = mybir.ActivationFunctionType
AX_X = mybir.AxisListType.X

P = 128
B, N, E = 4, 512, 512
H, D = 16, 32
HG = P // D
NG = H // HG
T = B * N
MB = N // P
EC = E // P
NX, TOPK, NGR, GTOP = 16, 4, 4, 2
GSZ = NX // NGR
FF = 256
FC = FF // P
ROUTE_SCALE = 2.5
EPS = 1e-5
TB = T // P
RT = T * TOPK // P + NX
NT = TB + RT
WC = 32
XW = E + WC
XS, WS = 1024.0, 256.0
QS = 64.0
HMAX = 4096.0
NC6 = EC + FC
HC = NC6 // 2
PIECE = HC * E // 2
JB = T // P
NCOL = NX * JB
CH = NCOL // P
NEG = 1.0e30


class Tile:

    def __init__(self, r, lo):
        self.r, self.lo, self.par = r, lo, lo % 2

    def at(self, d=0):
        return self.lo + d if self.r is None else self.r * 2 + (self.lo + d)

    def plus(self, d):
        return Tile(self.r, self.lo + d)

    def uses(self, d=0):
        return self.lo // 2 + 1 + d if self.r is None else self.r + (self.lo // 2 + 1 + d)

    def is_(self, n):
        return self.r is None and self.lo == n

    def below(self, n):
        return self.r is None and self.lo < n

    def shared(self):
        return self.lo < TB


def tile_pairs(eng, lo, hi, step):
    with eng.Fori(0, (hi - lo) // 2) as r:
        step(Tile(r, lo))
        step(Tile(r, lo + 1))


def constants():
    c = {}
    inv = (1.0 / np.float32(10000.0) ** (np.arange(0, D, 2, dtype=np.float32) / np.float32(D))).astype(np.float32)
    t = np.arange(N, dtype=np.float32)[:, None] * inv[None, :]
    cos, sin = np.cos(t).astype(np.float32), np.sin(t).astype(np.float32)
    lay = lambda a: a.reshape(MB, P, D).transpose(1, 0, 2)
    c["rope_cos"] = lay(np.concatenate([cos, cos], 1))
    c["rope_sin"] = lay(np.concatenate([-sin, sin], 1))
    c["ident"] = np.eye(P)
    c["ident16"] = np.eye(P)
    i = np.arange(P)
    c["causal"] = i[:, None] <= i[None, :]
    c["before"] = i[:, None] < i[None, :]
    e = np.arange(NX)
    c["tie16"] = np.tile((e[None, :] < e[:, None]).reshape(1, NX * NX), (P, 1))
    g = np.arange(NGR)
    c["tie4"] = np.tile((g[None, :] < g[:, None]).reshape(1, NGR * NGR), (P, 1))
    c["iota"] = np.tile(np.arange(NCOL)[None, :], (P, 1))
    col = np.arange(NCOL).reshape(CH, P).T
    c["col_piece"] = col % JB
    c["col_onehot"] = (col // JB)[:, :, None] == e[None, None, :]
    c["col_id"] = np.repeat((col // JB + 1)[:, :, None], P, 2)
    c["token"] = np.arange(1, T + 1).reshape(TB, P).T
    c["free_row"] = (T + 1 + np.arange(P))[:, None]
    return {k: np.ascontiguousarray(v.reshape(P, -1).astype(np.float32)) for k, v in c.items()}


def build(nc, x, w_qkv, w_out, ln_scale, ln_bias, gate_w, expert_bias, w_experts, cst, out):
    ctx = ExitStack()
    with ctx:
        sb = lambda n, s, d=F32: ctx.enter_context(nc.sbuf_tensor(n, s, d))
        sem = lambda n: ctx.enter_context(nc.semaphore(n))

        x1_dram = nc.dram_tensor("x1_scratch", [TB, P, E], F32, kind="Internal").ap()
        xn_dram = nc.dram_tensor("xn_scratch", [T + P, XW], I32, kind="Internal").ap()
        w16_dram = nc.dram_tensor("w16_scratch", [(NX + 1) * P, 2, NC6, E], F16, kind="Internal").ap()

        EW = EC * 2 * FF
        arena = sb("arena", [P, (NX + 1) * EW])
        EARLY = 5
        SPLIT = 3
        stage = arena[:, EARLY * EW:EARLY * EW + 2 * HC * E].rearrange("p (j n) -> p j n", j=2)
        halves = arena[:, EARLY * EW + 2 * HC * E:EARLY * EW + 4 * HC * E].bitcast(F16).rearrange(
            "p (j h n) -> p j h n", j=2, h=2)
        top = [(EARLY + SPLIT) * EW]

        def over(shape):
            n = int(np.prod(shape))
            a = arena[:, top[0]:top[0] + n]
            top[0] += n
            assert top[0] <= (NX + 1) * EW
            return a.rearrange("p (a b) -> p a b", a=shape[0]) if len(shape) == 2 else a

        gu = arena[:].bitcast(F16).rearrange("p (e h c n) -> p e h c n", e=NX + 1, h=2, c=EC)
        wqkv = over([EC, 3 * E])
        wout = over([EC, E])
        xnT = over([EC, N])
        q16, k16 = (over([NG, N]).bitcast(F16).rearrange("p g (h n) -> p h g n", h=2) for _ in range(2))
        s_sq = over([HG, N])
        xres = over([MB, E])
        C = {k: sb("c_" + k, [P, v.shape[1]]) for k, v in cst.items()}
        ident = C["ident"][:]
        ident16 = sb("ident16", [P, P], F16)
        ln_s, ln_b = sb("ln_s", [P, 1]), sb("ln_b", [P, 1])
        eps = sb("eps", [P, 1])
        ones = sb("ones", [P, P])
        gwT = sb("gwT", [P, EC, NX])
        ebias = sb("ebias", [P, NX])
        wrow = sb("wrow", [P, MB, WC])
        slot_tab = sb("slot_tab", [P, CH, P])
        seen = sb("seen", [P, MB + 1, NX])
        row_id = sb("row_id", [P, RT], I32)
        expert_id = sb("expert_id", [P, RT], I32)
        oh4 = sb("oh4", [P, MB * TOPK * NX])
        tmp4 = sb("tmp4", [P, MB])
        tile_hot = sb("tile_hot", [P, CH, RT])
        d16, d16i, d2 = sb("d16", [P, 2, NX]), sb("d16i", [P, 2, NX], I32), sb("d2", [P, 3, CH])
        free = sb("free", [P, RT])
        att = ExitStack()
        sa = lambda n, s, d=F32: att.enter_context(nc.sbuf_tensor(n, s, d))
        xin = sa("xin", [P, MB, E])
        vtok = sa("vtok", [P, MB, E])
        qkn = sa("qkn", [P, 2 * E])
        s_p4 = sa("s_p4", [P, 2, HG, N])
        t1, t2 = s_sq[:, 0:2, :].rearrange("p j n -> p (j n)"), s_sq[:, 2:4, :].rearrange("p j n -> p (j n)")
        xn2 = s_p4[:, 0]
        qk32 = s_p4[:, 1, 2:4, :]
        x2T = s_p4[:, 1, 0:2, :].rearrange("p j (c n) -> p j c n", c=EC)
        ra = sa("ra", [P, MB * TOPK, P], F16)
        rb = sa("rb", [P, MB * TOPK, NCOL], F16)
        cmp = rb[:].rearrange("p i n -> p (i n)").bitcast(F32)
        cmp1, cmp2 = cmp[:, 0:MB * NX * NX], cmp[:, MB * NX * NX:2 * MB * NX * NX]
        st = sa("st", [P, MB, 6])
        mv = sa("mv", [P, MB, 2])
        sd = sa("sd", [P, MB])
        logit = sa("logit", [P, MB * NX])
        first = sa("first", [P, 3, MB])
        hs = sa("hs", [P, 3, 2 * H])
        rec = qkn[:, 0:N]
        xn16 = vtok[:].rearrange("p m e -> p (m e)").bitcast(F16).rearrange("p (m h e) -> p m h e", m=MB, h=2)
        attT = xnT
        sc, bi, mb, rank, ws = (sa(n, [P, MB, NX]) for n in ("sc", "bi", "mb", "rank", "ws"))
        sel = sa("sel", [P, MB, NX])
        gp = sa("gp", [P, 8, MB * NGR * 2])
        ek = sa("ek", [P, MB, TOPK])
        ki = sa("ki", [P, 3, MB * TOPK], I32)
        kf = sa("kf", [P, 2, MB * TOPK])
        tok4 = sa("tok4", [P, MB])
        att.close()
        moe = ExitStack()
        sm = lambda n, s, d=F32: moe.enter_context(nc.sbuf_tensor(n, s, d))
        xg = sm("xg", [P, 2, XW], I32)
        hT = sm("hT", [P, 2, 2 * FC, P], F16)
        x1r = sm("x1r", [P, 2, E])
        wd = sm("wd", [P, 2, 2, FC, E], F16)
        xgT = sm("xgT", [P, 2, 2 * EC, P], F16)
        sg = sm("sg", [P, 2, FF])
        hh = sm("hh", [P, 2, FF])
        h16 = sm("h16", [P, 2, 2, FF], F16)
        hsc = sm("hsc", [P, 2, 4])
        yy = sm("yy", [P, 2, E])
        gidx = sm("gidx", [P, 2], I32)
        sidx = sm("sidx", [P, 2], I32)
        wr = sm("wr", [P, 2])
        moe.close()

        bank = [ctx.enter_context(nc.psum_tensor(f"bank{i}", [P, 512], F32)) for i in range(8)]
        quad = lambda bk: bk[:].rearrange("p (c n) -> p c n", c=4)
        oct16 = lambda bk: bk[:].bitcast(F16).rearrange("p (c n) -> p c n", c=8)

        consts_in, wqkv_in, wout_in, experts_in = map(sem, ("consts_in", "wqkv_in", "wout_in", "experts_in"))
        stage_in = [sem("stage_in0"), sem("stage_in1")]
        halves_out = [sem("halves_out0"), sem("halves_out1")]
        hi_done, lo_done, xhi_done, xn16_ready, up_used = map(sem, (
            "hi_done", "lo_done", "xhi_done", "xn16_ready", "up_used"))
        xin_in, xres_in, x1_out, xn2_out = map(sem, ("xin_in", "xres_in", "x1_out", "xn2_out"))
        memset_done = sem("memset_done")
        var1, std1, xn_ready = sem("var1"), sem("std1"), sem("xn_ready")
        xT_ps, xT_sb, qkv_ps = sem("xT_ps"), sem("xT_sb"), sem("qkv_ps")
        rope_parts, centred, squares, hvar, hstd, qkn_ready = map(sem, (
            "rope_parts", "centred", "squares", "hvar", "hstd", "qkn_ready"))
        v_sb, qkT_ps, qkT_sb = sem("v_sb"), sem("qkT_ps"), sem("qkT_sb")
        qk_lo, high_written, norm_known, logits_sb = map(sem, ("qk_lo", "high_written", "norm_known", "logits_sb"))
        p4_done = [sem("p4_done_even"), sem("p4_done_odd")]
        scores_ps, sq_done, p4_masked, pv_done, att_done = map(sem, (
            "scores_ps", "sq_done", "p4_masked", "pv_done", "att_done"))
        proj_ps, x1_ready, var2, std2, xn2_ready = map(sem, ("proj_ps", "x1_ready", "var2", "std2", "xn2_ready"))
        x2T_ps, x2T_sb, logits_ps, scores_sig, sel_ready, pos_ps, ab_ready, tab_ps = map(sem, (
            "x2T_ps", "x2T_sb", "logits_ps", "scores_sig", "sel_ready", "pos_ps", "ab_ready", "tab_ps"))
        count_ps, tiles_known, ids_ps, ids_ready = map(sem, (
            "count_ps", "tiles_known", "ids_ps", "ids_ready"))
        weights_ready, weights_out, zeros_out, weights_here = map(sem, (
            "weights_ready", "weights_out", "zeros_out", "weights_here"))
        numbers = sem("numbers")
        xg_in = [sem("xg_in0"), sem("xg_in1")]
        rows_in = [sem("rows_in0"), sem("rows_in1")]
        wd_in = [sem("wd_in0"), sem("wd_in1")]
        added = sem("added")
        gT_ps, gT_sb, gu_ps, silu_done, h_ready, hT_ps, hT_sb, y_ps, y_sb = map(sem, (
            "gT_ps", "gT_sb", "gu_ps", "silu_done", "h_ready", "hT_ps", "hT_sb", "y_ps", "y_sb"))
        x1r_in = [sem("x1r_in0"), sem("x1r_in1")]
        fin_out = [sem("fin_out0"), sem("fin_out1")]
        ident_in = sem("ident_in")
        NCST = len(cst) - 1 + 6

        block = ctx.enter_context(nc.Block())

        FIRST = 11
        def all_tiles(eng, step, routing):
            for t in range(FIRST):
                step(Tile(None, t))
                routing(t)
            tile_pairs(eng, FIRST, TB - 1, step)
            for t in range(TB - 1, TB + 3):
                step(Tile(None, t))
            tile_pairs(eng, TB + 3, NT - 1, step)
            step(Tile(None, NT - 1))

        @block.sync
        def _(sp):
            sp.dma_start(xin[:], x[0]).then_inc(xin_in, 16)
            sp.dma_start(C["ident"][:], cst["ident"]).then_inc(ident_in, 16)
            sp.dma_start(wqkv, w_qkv).then_inc(wqkv_in, 16)
            for k, v in cst.items():
                if k != "ident":
                    sp.dma_start(C[k][:], v).then_inc(consts_in, 16)
            for j in range(HG):
                if j < 2:
                    sp.dma_start(ln_s[64 * j:64 * j + 64, :], ln_scale[64 * j:64 * j + 64, :]).then_inc(consts_in, 16)
                else:
                    sp.dma_start(ln_b[64 * j - 128:64 * j - 64, :], ln_bias[64 * j - 128:64 * j - 64, :]).then_inc(consts_in, 16)
            sp.dma_start(gwT[:], gate_w).then_inc(consts_in, 16)
            sp.dma_start(ebias[:], expert_bias).then_inc(consts_in, 16)
            sp.dma_start(xres[:], x[0]).then_inc(xres_in, 16)
            sp.dma_start(wout, w_out).then_inc(wout_in, 16)
            sp.wait_ge(memset_done, 1)
            zeros = s_p4[:, 0, 0:2, :].rearrange("p j n -> p (j n)")
            sp.dma_start(xn_dram[T:T + P, :], zeros[:, 0:XW].bitcast(I32)).then_inc(weights_out, 16)
            sp.dma_start(out[T:T + P, :], zeros[:, 0:E]).then_inc(zeros_out, 16)

            def load_half(n):
                if n >= 2:
                    sp.wait_ge(lo_done, 2 * (n - 1))
                e, j = divmod(n, 2)
                sp.dma_start(stage[:, j], w_experts[e][:, j]).then_inc(stage_in[j], 16)

            def store_half(n):
                sp.wait_ge(lo_done, 2 * (n + 1))
                e, j = divmod(n, 2)
                sp.dma_start(w16_dram[e * P:e * P + P, :, HC * j:HC * j + HC, :].rearrange("p h c n -> p h (c n)"),
                             halves[:, j]).then_inc(halves_out[j], 16)

            def load_expert(e):
                sp.dma_start(gu[:, bass.ds(e, 1)].rearrange("p a h c n -> p (a h) (c n)"),
                             w16_dram[bass.ds(e * P, P), :, 0:EC, :].rearrange("p h c n -> p h (c n)")
                             ).then_inc(experts_in, 16)

            def store_weights(b):
                sp.wait_ge(weights_ready, b + 1)
                sp.dma_start(xn_dram[N * b:N * b + N, E:XW].rearrange("(m p) e -> p m e", p=P),
                             wrow[:].bitcast(I32)).then_inc(weights_out, 16)

            def load_rows(t):
                k = t.par
                if not t.below(2):
                    sp.wait_ge(gT_ps, t.at(-1))
                sp.dma_start(xg[:, k, 0:E], xn_dram[bass.ds(t.at() * P, P), 0:E]).then_inc(rows_in[k], 16)

            NH = 2 * (NX + 1)
            load_half(0)
            load_half(1)
            for b in range(B):
                sp.wait_ge(xT_ps, MB * (b + 1))
                sp.dma_start(xin[:], x[min(b + 1, B - 1)]).then_inc(xin_in, 16)
                for n in range(8 * b, 8 * b + 8):
                    store_half(n)
                    load_half(n + 2)
                if b == 2:
                    for j in range(2):
                        sp.wait_ge(halves_out[j], 16 * EARLY)
                    for e in range(EARLY):
                        load_expert(e)
                if b:
                    store_weights(b - 1)
                sp.wait_ge(x1_ready, MB * (b + 1))
                sp.dma_start(x1_dram[MB * b:MB * b + MB].rearrange("m p e -> p m e"), xres[:]).then_inc(x1_out, 16)
                if b == B - 1:
                    sp.wait_ge(xT_ps, MB * (B + 1))
                    sp.wait_ge(xn2_out, 16)
                    for t in range(2):
                        load_rows(Tile(None, t))
                sp.wait_ge(xn16_ready, b + 1)
                sp.dma_start(xn_dram[N * b:N * b + N, 0:E].rearrange("(m p) e -> p m e", p=P),
                             xn16.rearrange("p m h e -> p m (h e)").bitcast(I32)).then_inc(xn2_out, 16)
                if b + 1 < B:
                    sp.wait_ge(x1_out, 16 * (b + 1))
                    sp.dma_start(xres[:], x[b + 1]).then_inc(xres_in, 16)
            def load_residual(t):
                sp.dma_start(x1r[:, t.par], x1_dram[bass.ds(t.at(), 1)].rearrange("m p e -> p (m e)")
                             ).then_inc(x1r_in[t.par], 16)

            def store_result(t):
                sp.wait_ge(y_sb, t.at(1))
                sp.dma_start(out[bass.ds(t.at() * P, P), :], yy[:, t.par]).then_inc(fin_out[t.par], 16)

            def load_down(t):
                k = t.par
                if not t.below(2):
                    sp.wait_ge(y_ps, t.at(-1))
                e = 0 if t.shared() else sp.value_load(expert_id[0:1, bass.ds(t.at(-TB), 1)], min_val=0, max_val=NX)
                sp.dma_start(wd[:, k].rearrange("p h c n -> p h (c n)"),
                             w16_dram[bass.ds(e * P, P), :, EC:NC6, :].rearrange("p h c n -> p h (c n)")
                             ).then_inc(wd_in[k], 16)

            def shared_step(t):
                if t.r is not None or t.lo < TB - 2:
                    load_rows(t.plus(2))
                if not t.below(3):
                    store_result(t.plus(-3))
                    load_residual(t.plus(-1))

            def shared_and_expert(t):
                shared_step(t)
                load_expert(t.at(EARLY + SPLIT - 1))

            sp.wait_ge(proj_ps, MB * B)
            sp.wait_ge(xT_sb, MB * (B + 1))
            sp.wait_ge(x1_out, 16 * B)
            sp.wait_ge(xn2_out, 16 * B)
            for t in range(2):
                load_down(Tile(None, t))
                load_residual(Tile(None, t))
            shared_step(Tile(None, 0))
            APART = NX - EARLY - SPLIT
            for t in (1, 2):
                shared_and_expert(Tile(None, t))
            tile_pairs(sp, 3, 1 + APART, shared_and_expert)
            for n in range(NH - 2, NH):
                store_half(n)
            for j in range(2):
                sp.wait_ge(halves_out[j], 16 * (NX + 1))
            for t in range(1 + APART, TB + 1):
                shared_step(Tile(None, t))
                if t - 1 - APART < SPLIT:
                    load_expert(EARLY + t - 1 - APART)
                elif t - 1 - APART == SPLIT:
                    load_expert(NX)
                    store_weights(B - 1)
            sp.wait_ge(ids_ready, 1)
            load_down(Tile(None, TB))
            store_result(Tile(None, TB - 2))
            load_down(Tile(None, TB + 1))
            store_result(Tile(None, TB - 1))
            tile_pairs(sp, TB + 2, NT, load_down)

        @block.tensor
        def _(pe):
            pe.wait_ge(ident_in, 16)
            def transposed_rows(b, src, ready, m, done, copied):
                pe.wait_ge(ready, b * MB + (m + 1))
                if m >= 2:
                    pe.wait_ge(copied, b * MB + (m - 1))
                for c in range(EC):
                    mm = pe.transpose(quad(bank[4 + m % 2])[:, c], src[:, m, c * P:c * P + P], ident)
                mm.then_inc(done, 1)

            def qkv(b, m):
                pe.wait_ge(xT_sb, b * MB + (m + 1))
                for w in range(3):
                    if m:
                        pe.wait_ge(*((rope_parts, b * MB + m) if w < 2 else (v_sb, b * MB + m)))
                    for c in range(EC):
                        mm = pe.matmul(bank[w][:], xnT[:, c, m * P:m * P + P], wqkv[:, c, w * E:w * E + E],
                                       start=(c == 0), stop=(c == EC - 1))
                    mm.then_inc(qkv_ps, 1)

            def qk_transposes(b, m):
                pe.wait_ge(qkn_ready, b * MB + (m + 1))
                if m:
                    pe.wait_ge(qkT_sb, b * (2 * MB) + 2 * m)
                for w in range(2):
                    for g in range(NG):
                        mm = pe.transpose(quad(bank[6 + w])[:, g], qkn[:, w * E + g * P:w * E + g * P + P], ident)
                    mm.then_inc(qkT_ps, 1)

            def logits(b, m):
                pe.wait_ge(x2T_sb, b * MB + (m + 1))
                for c in range(EC):
                    mm = pe.matmul(bank[3][:, m * NX:m * NX + NX], x2T[:, m % 2, c, :], gwT[:, c, :],
                                   start=(c == 0), stop=(c == EC - 1))
                if m == MB - 1:
                    mm.then_inc(logits_ps, 1)

            def places(b, bk=bank[4]):
                pe.wait_ge(sel_ready, b + 1)
                for m in range(MB):
                    o = bk[:, m * NX:m * NX + NX]
                    pe.matmul(o, C["before"][:], sel[:, m, :], start=True, stop=False)
                    mm = pe.matmul(o, ones[:], seen[:, m, :], start=False, stop=True)
                mm.then_inc(pos_ps, 1)

            def table(b, bk=bank[5]):
                pe.wait_ge(ab_ready, b + 1)
                for h in range(CH):
                    for i in range(MB * TOPK):
                        mm = pe.matmul(bk[:, h * P:h * P + P], rb[:, i, h * P:h * P + P], ra[:, i, :],
                                       start=(i == 0), stop=(i == MB * TOPK - 1))
                mm.then_inc(tab_ps, 1)

            def sequence(b, before):
                if before is not None:
                    pe.wait_ge(x1_ready, b * MB)
                pe.wait_ge(wqkv_in, 16)
                pe.wait_ge(consts_in, 16 * NCST)
                pe.wait_ge(memset_done, 1)
                for m in range(MB):
                    qkv(b, m)
                    if m:
                        qk_transposes(b, m - 1)
                    if before is not None and m == 2:
                        pe.wait_ge(xT_sb, b * MB + MB)
                        for k in range(2):
                            transposed_rows(before, xn2, xn2_ready, k, x2T_ps, x2T_sb)
                if before is not None:
                    logits(before, 0)
                    for m in range(2, MB):
                        transposed_rows(before, xn2, xn2_ready, m, x2T_ps, x2T_sb)
                        logits(before, m - 1)
                    logits(before, MB - 1)
                qk_transposes(b, MB - 1)
                pe.wait_ge(qk_lo, b * (2 * MB) + 2 * MB)
                pe.wait_ge(v_sb, b * MB + MB)
                for i in range(NG * MB + 1):
                    if i < NG * MB:
                        g, kb = divmod(i, MB)
                        order = [(n, j) for n in range(3) for j in range(HG)]
                        for n, j in order:
                            if i and n == 0:
                                pe.wait_ge(sq_done, b * (NG * MB * HG) + (HG * (i - 1) + j + 1))
                            if i == 0 and n == 0 and j == 3 and before is not None:
                                pe.wait_ge(logits_sb, b)
                            r, kh, qh = slice(D * j, D * j + D), n // 2, n % 2
                            mm = pe.matmul(bank[j][:, 0:N - P * kb], k16[r, kh, g, P * kb:P * kb + P],
                                           q16[r, qh, g, P * kb:N], start=(n == 0), stop=(n == 2))
                            if n == 2:
                                mm.then_inc(scores_ps, 1)
                    if i:
                        g, kb = divmod(i - 1, MB)
                        if kb == 0 and g:
                            pe.wait_ge(att_done, b * NG + g)
                        for n in range(2):
                            for j in range(HG):
                                if n == 0:
                                    pe.wait_ge(p4_masked, b * (NG * MB * HG) + (HG * (i - 1) + j + 1))
                                r = slice(D * j, D * j + D)
                                w = vtok[:, kb, (g * HG + j) * D:(g * HG + j) * D + D] if n == 0 else ones[:, 0:D]
                                mm = pe.matmul(bank[6 + n][r, P * kb:N], w, s_p4[:, (i - 1) % 2, j, 0:N - P * kb],
                                               start=(kb == 0), stop=(kb == MB - 1), skip_group_check=True)
                        mm.then_inc(pv_done, 1)
                    if before is not None:
                        if i == 7:
                            places(before)
                        if i == 15:
                            table(before)
                pe.wait_ge(wout_in, 16)
                pe.wait_ge(sq_done, b * (NG * MB * HG) + NG * MB * HG)
                for g in range(NG):
                    pe.wait_ge(att_done, b * NG + (g + 1))
                    for m in range(MB):
                        mm = pe.matmul(bank[m][:], attT[:, g, m * P:m * P + P], wout[:, g, :],
                                       start=(g == 0), stop=(g == NG - 1))
                        if g == NG - 1:
                            mm.then_inc(proj_ps, 1)
                for m in range(MB):
                    if m == 1 and before is not None:
                        pe.wait_ge(x1_ready, b * MB + 1)
                    transposed_rows(b + 1, xin, xn_ready, m, xT_ps, xT_sb)

            for m in range(MB):
                transposed_rows(0, xin, xn_ready, m, xT_ps, xT_sb)
            sequence(0, None)
            with pe.Fori(0, B - 1) as r:
                sequence(r + 1, r)
            pe.wait_ge(xT_sb, MB * (B + 1))
            for m in range(MB):
                transposed_rows(B - 1, xn2, xn2_ready, m, x2T_ps, x2T_sb)
                if m:
                    logits(B - 1, m - 1)
            logits(B - 1, MB - 1)
            def gather_T(t):
                k = t.par
                if t.shared():
                    pe.wait_ge(rows_in[k], t.uses() * 16)
                else:
                    pe.wait_ge(xg_in[k], t.plus(-TB).uses() * 16)
                if not t.below(2):
                    pe.wait_ge(gT_sb, t.at(-1))
                for c in range(2 * EC):
                    mm = pe.transpose(oct16(bank[k])[:, c], xg[:, k, 0:E].bitcast(F16)[:, c * P:c * P + P], ident16[:])
                mm.then_inc(gT_ps, 1)

            def gate_up(t, e, chunks):
                k = t.par
                for c in chunks:
                    for xh, wh in ((0, 0), (0, 1), (1, 0)):
                        w = gu[:, 0, wh, c, :] if e is None else gu[:, bass.ds(e, 1), wh, c, :]
                        mm = pe.matmul(bank[2 + k][:], xgT[:, k, xh * EC + c, :], w,
                                       start=(c == 0 and xh + wh == 0), stop=(c == EC - 1 and xh == 1))
                return mm

            def hidden_T(t):
                k = t.par
                pe.wait_ge(h_ready, t.at(1))
                if not t.below(1):
                    pe.wait_ge(hT_sb, t.at())
                for c in range(2 * FC):
                    mm = pe.transpose(oct16(bank[4])[:, c], h16[:, k, c // FC, (c % FC) * P:(c % FC) * P + P], ident16[:])
                mm.then_inc(hT_ps, 1)

            def down(t):
                k = t.par
                pe.wait_ge(hT_sb, t.at(1))
                pe.wait_ge(wd_in[k], 16 if t.shared() else t.plus(-TB).uses(1) * 16)
                if not t.below(2):
                    pe.wait_ge(y_sb, t.at(-1))
                for c in range(FC):
                    for hh_, wh in ((0, 0), (0, 1), (1, 0)):
                        mm = pe.matmul(bank[5 + k][:], hT[:, k, hh_ * FC + c, :], wd[:, k, wh, c, :],
                                       start=(c == 0 and hh_ + wh == 0), stop=(c == FC - 1 and hh_ == 1))
                mm.then_inc(y_ps, 1)

            def step(t):
                if t.is_(TB):
                    pe.wait_ge(ids_ready, 1)
                    pe.wait_ge(experts_in, 16 * (NX + 1))
                e = None if t.shared() else pe.value_load(expert_id[0:1, bass.ds(t.at(-TB), 1)], min_val=0, max_val=NX)
                pe.wait_ge(gT_sb, t.at(1))
                if not t.below(2):
                    pe.wait_ge(h_ready, t.at(-1))
                gate_up(t, e, range(EC - 1))
                if not t.is_(0):
                    hidden_T(t.plus(-1))
                gate_up(t, e, range(EC - 1, EC)).then_inc(gu_ps, 1)
                if not t.is_(NT - 1):
                    gather_T(t.plus(1))
                if not t.is_(0):
                    down(t.plus(-1))

            def routing(t):
                if t == 3:
                    places(B - 1, bank[7])
                elif t == 7:
                    table(B - 1, bank[7])
                elif t == 9:
                    pe.wait_ge(sel_ready, B + 1)
                    pe.matmul(bank[7][:, 0:NX], ones[:], seen[:, 0, :], start=True, stop=True).then_inc(count_ps, 1)
                elif t == 10:
                    pe.wait_ge(tiles_known, 1)
                    for h in range(CH):
                        pe.matmul(bank[7][:, 0:RT], slot_tab[:, h, :], tile_hot[:, h, :], start=(h == 0), stop=(h == CH - 1))
                    for h in range(CH):
                        mm = pe.matmul(bank[7][:, RT:2 * RT], C["col_id"][:, h * P:h * P + P], tile_hot[:, h, :],
                                       start=(h == 0), stop=(h == CH - 1))
                    mm.then_inc(ids_ps, 1)

            pe.wait_ge(experts_in, 16 * EARLY)
            gather_T(Tile(None, 0))
            all_tiles(pe, step, routing)
            hidden_T(Tile(None, NT - 1))
            down(Tile(None, NT - 1))

        @block.scalar
        def _(act):
            act.wait_ge(memset_done, 1)

            def split_hi(j, q, n):
                a = slice(q * PIECE, q * PIECE + PIECE)
                act.activation(halves[:, j, 0, a], stage[:, j, a], ACT.Copy, scale=WS).then_inc(high_written, 1)
                act.wait_ge(high_written, n)
                act.activation(stage[:, j, a], stage[:, j, a], ACT.Copy, scale=WS).then_inc(hi_done, 1)

            def split_next(b, i):
                j, q = i // 2 % 2, i % 2
                if q == 0:
                    act.wait_ge(stage_in[j], b * (16 * MB) + 16 * (i // 4 + 1))
                    if i >= 4 or not isinstance(b, int):
                        act.wait_ge(halves_out[j], b * (16 * MB) + 16 * (i // 4))
                split_hi(j, q, b * (NG * MB) + (i + 1))

            def copy_rows(b, m):
                act.wait_ge(x2T_ps, b * MB + (m + 1))
                act.activation(x2T[:, m % 2], quad(bank[4 + m % 2]), ACT.Copy).then_inc(x2T_sb, 1)

            def copy_logits(b):
                act.wait_ge(logits_ps, b + 1)
                act.activation(logit[:], bank[3][:, 0:MB * NX], ACT.Copy).then_inc(logits_sb, 1)

            def gate_scores(b):
                act.wait_ge(logits_sb, b + 1)
                act.activation(sc[:].rearrange("p m e -> p (m e)"), logit[:], ACT.Sigmoid).then_inc(scores_sig, 1)

            def qkT(b, m):
                for w, dst in enumerate((q16, k16)):
                    act.wait_ge(qkT_ps, b * (2 * MB) + (2 * m + w + 1))
                    act.activation(dst[:, 0, :, m * P:m * P + P], quad(bank[6 + w]), ACT.Identity,
                                   bias=ln_b[:, 0:1], scale=ln_s[:, 0:1])
                    if m or not isinstance(b, int):
                        act.wait_ge(qk_lo, b * (2 * MB) + (2 * m + w - 1))
                    act.activation(qk32[:, w, :].rearrange("p (c n) -> p c n", c=4), quad(bank[6 + w]), ACT.Identity,
                                   bias=ln_b[:, 0:1], scale=ln_s[:, 0:1]).then_inc(qkT_sb, 1)

            def deviation(n):
                act.wait_ge(var1, n)
                act.activation(first[:, 0, :], mv[:, :, 1], ACT.Sqrt, bias=eps[:, 0:1]).then_inc(std1, 1)

            def first_norm(n):
                act.wait_ge(norm_known, n)
                for m in range(MB):
                    act.activation(xin[:, m, :], xin[:, m, :], ACT.Identity, bias=first[:, 2, m:m + 1],
                                   scale=first[:, 1, m:m + 1]).then_inc(xn_ready, 1)

            def copy_first(b, m):
                act.wait_ge(xT_ps, b * MB + (m + 1))
                act.activation(xnT[:, :, m * P:m * P + P], quad(bank[4 + m % 2]), ACT.Copy).then_inc(xT_sb, 1)

            def sequence(b, before):
                for m in range(MB):
                    act.wait_ge(qkv_ps, b * (3 * MB) + (3 * m + 3))
                    if m == 0 and before is not None:
                        act.wait_ge(xn2_out, b * 16)
                    act.activation(vtok[:, m, :], bank[2][:], ACT.Copy).then_inc(v_sb, 1)
                    if m:
                        qkT(b, m - 1)
                    if before is not None and m == MB - 1:
                        copy_rows(before, 0)
                        copy_rows(before, 1)
                    act.wait_ge(centred, b * MB + (m + 1))
                    act.activation(t2, t1, ACT.Square).then_inc(squares, 1)
                    act.wait_ge(hvar, b * MB + (m + 1))
                    act.activation(hs[:, 1, :], hs[:, 0, :], ACT.Sqrt, bias=eps[:, 0:1], scale=1.0 / D).then_inc(hstd, 1)
                if before is not None:
                    copy_rows(before, 2)
                    copy_rows(before, 3)
                qkT(b, MB - 1)
                if before is not None:
                    copy_logits(before)

                def fourth(i, j):
                    act.wait_ge(sq_done, b * (NG * MB * HG) + (HG * i + j + 1))
                    if i >= 2:
                        act.wait_ge(pv_done, b * (NG * MB) + (i - 1))
                    w = N - P * (i % MB)
                    act.activation(s_p4[:, i % 2, j, 0:w], s_sq[:, j, 0:w], ACT.Square).then_inc(p4_done[1], 1)

                for i in range(NG * MB):
                    kb = i % MB
                    for j in range(HG):
                        act.wait_ge(scores_ps, b * (NG * MB * HG) + (HG * i + j + 1))
                        if i:
                            act.wait_ge(p4_done[j % 2], b * (NG * MB * 2) + (2 * i - 1 + j // 2))
                        act.activation(s_sq[:, j, 0:N - P * kb], bank[j][:, 0:N - P * kb], ACT.Square,
                                       scale=1.0 / (QS * QS)).then_inc(sq_done, 1)
                        if j == 2:
                            fourth(i, 1)
                    fourth(i, 3)
                    if i == 0 and before is not None:
                        gate_scores(before)
                    split_next(b, i)
                    if i == 13:
                        deviation(b + 2)
                    if i == 14:
                        first_norm(b + 2)
                copy_first(b + 1, 0)
                copy_first(b + 1, 1)
                act.wait_ge(var2, b + 1)
                act.activation(sd[:], mv[:, :, 1], ACT.Sqrt, bias=eps[:, 0:1]).then_inc(std2, 1)
                copy_first(b + 1, 2)
                copy_first(b + 1, 3)
                for m in range(MB):
                    act.wait_ge(xn2_ready, b * MB + (m + 1))
                    act.activation(xn16[:, m, 0, :], xn2[:, m, :], ACT.Copy, scale=XS).then_inc(xhi_done, 1)

            deviation(1)
            first_norm(1)
            for m in range(MB):
                copy_first(0, m)
            act.wait_ge(consts_in, 16 * NCST)
            sequence(0, None)
            with act.Fori(0, B - 1) as r:
                sequence(r + 1, r)
            for m in range(MB):
                copy_rows(B - 1, m)
            copy_logits(B - 1)
            gate_scores(B - 1)

            def copy_hidden(t):
                k = t.par
                act.wait_ge(hT_ps, t.at(1))
                if not t.below(2):
                    act.wait_ge(y_ps, t.at(-1))
                act.activation(hT[:, k], oct16(bank[4])[:, 0:2 * FC], ACT.Copy).then_inc(hT_sb, 1)

            def copy_T(t):
                k = t.par
                act.wait_ge(gT_ps, t.at(1))
                if not t.below(2):
                    act.wait_ge(gu_ps, t.at(-1))
                act.activation(xgT[:, k], oct16(bank[k]), ACT.Copy).then_inc(gT_sb, 1)

            def step(t):
                k = t.par
                if not t.is_(0):
                    copy_hidden(t.plus(-1))
                act.wait_ge(gu_ps, t.at(1))
                if not t.below(2):
                    act.wait_ge(up_used, t.at(-1))
                act.activation(sg[:, k], bank[2 + k][:, 0:FF], ACT.Silu, scale=1.0 / (XS * WS)).then_inc(silu_done, 1)
                if not t.is_(NT - 1):
                    copy_T(t.plus(1))

            act.wait_ge(xn16_ready, B)
            copy_T(Tile(None, 0))
            all_tiles(act, step, lambda t: split_next(B, t) if t < 4 else None)
            copy_hidden(Tile(None, NT - 1))

        @block.gpsimd
        def _(pool):
            pool.memset(eps[:], EPS)
            pool.memset(ones[:], 1.0)
            pool.memset(seen[:, 0, :], 0.0)
            pool.memset(slot_tab[:], 0.0)
            pool.memset(wrow[:], 0.0)
            pool.memset(s_p4[:, 0, 0:2, :], 0.0)
            pool.drain()
            pool.memset(tile_hot[:], 0.0).then_inc(memset_done, 1)
            pool.wait_ge(consts_in, 16 * NCST)
            def sequence(b):
                for i in range(NG * MB):
                    for j in range(HG):
                        pool.wait_ge(p4_done[j % 2], b * (NG * MB * 2) + (2 * i + j // 2 + 1))
                        d = s_p4[:, i % 2, j, 0:P]
                        pool.tensor_tensor(d, d, C["causal"][:], ALU.mult).then_inc(p4_masked, 1)
                    split_lo(b, i)

            def split_lo(b, i):
                j, q = i // 2 % 2, i % 2
                a = slice(q * PIECE, q * PIECE + PIECE)
                pool.wait_ge(hi_done, b * (NG * MB) + (i + 1))
                pool.tensor_tensor(halves[:, j, 1, a], stage[:, j, a], halves[:, j, 0, a], ALU.subtract
                                   ).then_inc(lo_done, 1)

            sequence(0)
            with pool.Fori(0, B - 1) as r:
                sequence(r + 1)
            for i in range(4):
                split_lo(B, i)

            def weight(t):
                k = t.par
                pool.wait_ge(gT_ps, t.at(1))
                pool.wait_ge(h_ready, t.at(-1))
                e = pool.value_load(expert_id[0:1, bass.ds(t.at(-TB), 1)], min_val=0, max_val=NX)
                pool.tensor_copy(wr[:, k:k + 1], xg[:, k, E:XW].bitcast(F32)[:, bass.ds(e, 1)]
                                 ).then_inc(weights_here, 1)

            def gather_numbers(t, again=False):
                if not t.below(TB + 2):
                    pool.wait_ge(xg_in[t.par], t.plus(-TB).uses(0 if again else -1) * 16)
                pool.tensor_copy(gidx[:, t.par:t.par + 1], row_id[:, bass.ds(t.at(-TB), 1)]).then_inc(numbers, 1)

            def scatter_numbers(t):
                pool.tensor_copy(sidx[:, t.par:t.par + 1], row_id[:, bass.ds(t.at(-TB), 1)]).then_inc(numbers, 1)

            def gather(t):
                k = t.par
                pool.indirect_dma_start(out=xg[:, k], out_offset=None, in_=xn_dram,
                                        in_offset=bass.IndirectOffsetOnAxis(ap=gidx[:, k:k + 1], axis=0)
                                        ).then_inc(xg_in[k], 16)

            def scatter(t):
                k = t.par
                pool.indirect_dma_start(out=out, out_offset=bass.IndirectOffsetOnAxis(ap=sidx[:, k:k + 1], axis=0),
                                        in_=yy[:, k], in_offset=None, compute_op=ALU.add).then_inc(added, 16)

            def weight_and_rows(t):
                weight(t.plus(-2))
                pool.wait_ge(weights_here, t.at(-1 - TB))
                pool.wait_ge(numbers, t.at(-1 - TB) * 2 if not t.below(TB + 4) else t.at(2 - TB))
                if t.is_(NT - 1):
                    gather_numbers(t.plus(-1), again=True)
                else:
                    gather_numbers(t.plus(1))
                gather(t)

            def step(t):
                weight_and_rows(t)
                pool.wait_ge(y_sb, t.at(-3))
                pool.wait_ge(added, t.at(-4 - TB) * 16)
                scatter_numbers(t.plus(-3))
                scatter(t.plus(-4))

            pool.wait_ge(ids_ready, 1)
            gather_numbers(Tile(None, TB))
            pool.wait_ge(xn2_out, 16 * B)
            pool.wait_ge(weights_out, 16 * (B + 1))
            pool.wait_ge(gT_ps, TB - 1)
            pool.wait_ge(numbers, 1)
            gather_numbers(Tile(None, TB + 1))
            gather(Tile(None, TB))
            pool.wait_ge(gT_ps, TB)
            pool.wait_ge(numbers, 2)
            scatter_numbers(Tile(None, TB))
            gather(Tile(None, TB + 1))
            gather_numbers(Tile(None, TB + 2))
            for t in range(TB + 2, TB + 4):
                weight_and_rows(Tile(None, t))
            for k in range(2):
                pool.wait_ge(fin_out[k], 16 * TB // 2)
            pool.wait_ge(zeros_out, 16)
            t = Tile(None, TB + 4)
            weight_and_rows(t)
            pool.wait_ge(y_sb, t.at(-3))
            scatter_numbers(t.plus(-3))
            scatter(t.plus(-4))
            step(Tile(None, TB + 5))
            tile_pairs(pool, TB + 6, NT - 2, step)
            step(Tile(None, NT - 2))
            step(Tile(None, NT - 1))
            for t in range(NT, NT + 4):
                t = Tile(None, t)
                if t.below(NT + 2):
                    weight(t.plus(-2))
                pool.wait_ge(y_sb, t.at(-3))
                pool.wait_ge(added, t.at(-4 - TB) * 16)
                pool.wait_ge(numbers, RT + t.at(-2 - TB))
                if t.below(NT + 3):
                    scatter_numbers(t.plus(-3))
                else:
                    gather_numbers(t.plus(-4), again=True)
                scatter(t.plus(-4))
            pool.wait_ge(added, 16 * RT)

        @block.vector
        def _(dve):
            heads = lambda a: a.rearrange("p (h d) -> p h d", d=D)
            per_head = lambda a: a.unsqueeze(2).to_broadcast([P, 2 * H, D])

            def norm_stats(m, src, last):
                dve.bn_stats(st[:, m, :], src[:, m, :])
                if last is not None:
                    dve.drain()
                    for k in range(MB):
                        i = dve.bn_aggr(mv[:, k, :], st[:, k, :])
                    i.then_inc(last, 1)

            def normed(dst, src, ready):
                dve.reciprocal(sd[:], sd[:])
                dve.drain()
                for m in range(MB):
                    dve.tensor_scalar(dst[:, m, :], src[:, m, :], mv[:, m, 0:1], sd[:, m:m + 1],
                                      ALU.subtract, ALU.mult).then_inc(ready, 1)

            fl = lambda a: a.rearrange("p m e -> p (m e)")
            n1, n2 = MB * NGR, MB * NGR * 2
            oh = oh4[:].rearrange("p (m k e) -> p m k e", m=MB, k=TOPK)
            row = lambda a: a.unsqueeze(2).to_broadcast([P, MB, TOPK, NX])
            member = lambda a: a.unsqueeze(2).to_broadcast([P, n1, GSZ])
            groups = lambda a: fl(a).rearrange("p (g s) -> p g s", s=GSZ)

            def compare(val, n):
                q = "p (m e f) -> p m e f"
                c1 = cmp1[:, 0:MB * n * n].rearrange(q, m=MB, e=n)
                c2 = cmp2[:, 0:MB * n * n].rearrange(q, m=MB, e=n)
                f = val.unsqueeze(2).to_broadcast([P, MB, n, n])
                e = val.unsqueeze(3).to_broadcast([P, MB, n, n])
                dve.tensor_tensor(c1, f, e, ALU.is_gt)
                dve.tensor_tensor(c2, f, e, ALU.is_equal)
                dve.drain()

            def ranks(dst, n, tie):
                q = "p (m e f) -> p m e f"
                c1 = cmp1[:, 0:MB * n * n].rearrange(q, m=MB, e=n)
                c2 = cmp2[:, 0:MB * n * n].rearrange(q, m=MB, e=n)
                dve.tensor_tensor(c2, c2, tie.rearrange("p (e f) -> p e f", e=n).unsqueeze(1).to_broadcast(
                    [P, MB, n, n]), ALU.mult)
                dve.drain()
                dve.tensor_tensor(c1, c1, c2, ALU.add)
                dve.drain()
                dve.tensor_reduce(dst, c1, AX_X, ALU.add)
                dve.drain()

            def group_sums(b):
                dve.tensor_copy(tok4[:], C["token"][:, bass.ds(b * MB, MB)])
                dve.wait_ge(scores_sig, b + 1)
                dve.tensor_tensor(bi[:], sc[:], ebias[:].unsqueeze(1).to_broadcast([P, MB, NX]), ALU.add)
                dve.drain()
                pr = fl(bi[:]).rearrange("p (g two) -> p g two", two=2)
                dve.tensor_tensor(gp[:, 0, 0:n2], pr[:, :, 0], pr[:, :, 1], ALU.max)
                dve.tensor_tensor(gp[:, 1, 0:n2], pr[:, :, 0], pr[:, :, 1], ALU.min)
                dve.drain()
                mx = gp[:, 0, 0:n2].rearrange("p (g two) -> p g two", two=2)
                mn = gp[:, 1, 0:n2].rearrange("p (g two) -> p g two", two=2)
                dve.tensor_tensor(gp[:, 2, 0:n1], mx[:, :, 0], mx[:, :, 1], ALU.max)
                dve.tensor_tensor(gp[:, 3, 0:n1], mx[:, :, 0], mx[:, :, 1], ALU.min)
                dve.tensor_tensor(gp[:, 4, 0:n1], mn[:, :, 0], mn[:, :, 1], ALU.max)
                dve.drain()
                dve.tensor_tensor(gp[:, 5, 0:n1], gp[:, 3, 0:n1], gp[:, 4, 0:n1], ALU.max)
                dve.drain()
                dve.tensor_tensor(gp[:, 6, 0:n1], gp[:, 2, 0:n1], gp[:, 5, 0:n1], ALU.add)
                dve.drain()


            def group_choice():
                gs = gp[:, 6, 0:n1].rearrange("p (m g) -> p m g", m=MB)
                compare(gs, NGR)
                ranks(gp[:, 7, 0:n1].rearrange("p (m g) -> p m g", m=MB), NGR, C["tie4"][:])
                dve.tensor_scalar(gp[:, 5, 0:n1], gp[:, 7, 0:n1], float(GTOP), None, ALU.is_lt)
                dve.drain()
                dve.tensor_scalar(gp[:, 4, 0:n1], gp[:, 5, 0:n1], NEG, -NEG, ALU.mult, ALU.add)
                dve.tensor_tensor(groups(mb[:]), groups(bi[:]), member(gp[:, 5, 0:n1]), ALU.mult)
                dve.drain()
                dve.tensor_tensor(groups(mb[:]), groups(mb[:]), member(gp[:, 4, 0:n1]), ALU.add)
                dve.drain()

            def expert_choice():
                ranks(rank[:], NX, C["tie16"][:])
                dve.tensor_scalar(sel[:], rank[:], float(TOPK), None, ALU.is_lt)
                dve.drain()
                for m in range(MB):
                    i = dve.tensor_tensor(seen[:, m + 1, :], seen[:, m, :], sel[:, m, :], ALU.add)
                    if m == MB - 1:
                        i.then_inc(sel_ready, 1)
                    dve.drain()

            def choice_weights(b):
                dve.tensor_tensor(ws[:], sc[:], sel[:], ALU.mult)
                dve.drain()
                dve.tensor_reduce(tmp4[:, 0:MB], ws[:], AX_X, ALU.add)
                dve.drain()
                dve.tensor_scalar(tmp4[:, 0:MB], tmp4[:, 0:MB], 1e-20, None, ALU.add)
                dve.drain()
                dve.reciprocal(tmp4[:, 0:MB], tmp4[:, 0:MB])
                dve.drain()
                dve.tensor_tensor(ws[:], ws[:], tmp4[:, 0:MB].unsqueeze(2).to_broadcast([P, MB, NX]), ALU.mult)
                dve.drain()
                dve.wait_ge(weights_out, b * 16 + 16)
                dve.tensor_scalar(wrow[:, :, 1:NX + 1], ws[:], ROUTE_SCALE, None, ALU.mult).then_inc(weights_ready, 1)
                oh = oh4[:].rearrange("p (m k e) -> p m k e", m=MB, k=TOPK)
                dve.tensor_tensor(oh, rank[:].unsqueeze(2).to_broadcast([P, MB, TOPK, NX]),
                                  C["iota"][:, 0:TOPK].unsqueeze(1).unsqueeze(3).to_broadcast([P, MB, TOPK, NX]), ALU.is_equal)
                dve.drain()


            def chosen(dst, val):
                c1 = cmp1[:, 0:MB * TOPK * NX].rearrange("p (m k e) -> p m k e", m=MB, k=TOPK)
                dve.tensor_tensor(c1, oh, val, ALU.mult)
                dve.drain()
                dve.tensor_reduce(dst, c1, AX_X, ALU.add)
                dve.drain()


            def choice_values():
                chosen(ek[:], C["iota"][:, 0:NX].unsqueeze(1).unsqueeze(1).to_broadcast([P, MB, TOPK, NX]))

            def choice_places(b, bk=bank[4]):
                dve.wait_ge(pos_ps, b + 1)
                pk = kf[:, 0, :].rearrange("p (m k) -> p m k", m=MB)
                chosen(pk, row(bk[:, 0:MB * NX].rearrange("p (m e) -> p m e", m=MB)))
                dve.tensor_copy(seen[:, 0, :], seen[:, MB, :])
                dve.tensor_copy(ki[:, 0, :], kf[:, 0, :])
                dve.drain()
                dve.tensor_scalar(ki[:, 1, :], ki[:, 0, :], P - 1, None, ALU.bitwise_and)
                dve.tensor_scalar(ki[:, 2, :], ki[:, 0, :], P.bit_length() - 1, None, ALU.logical_shift_right)
                dve.drain()
                dve.tensor_copy(kf[:, 0, :], ki[:, 1, :])
                dve.tensor_copy(kf[:, 1, :], ki[:, 2, :])
                dve.drain()
                dve.scalar_tensor_tensor(out=kf[:, 1, :], in0=ek[:].rearrange("p m k -> p (m k)"), scalar=float(JB),
                                         in1=kf[:, 1, :], op0=ALU.mult, op1=ALU.add)
                dve.drain()

            def place_rows(m):
                for i in range(m * TOPK, m * TOPK + TOPK):
                    dve.tensor_scalar(ra[:, i, :], C["iota"][:, 0:P], kf[:, 0, i:i + 1], None, ALU.is_equal)
                    k = dve.tensor_scalar(rb[:, i, :], C["iota"][:], kf[:, 1, i:i + 1], tok4[:, i // TOPK:i // TOPK + 1],
                                          ALU.is_equal, ALU.mult)
                if m == MB - 1:
                    k.then_inc(ab_ready, 1)

            def add_table(b, bk=bank[5]):
                dve.wait_ge(tab_ps, b + 1)
                dve.tensor_tensor(slot_tab[:].rearrange("p h r -> p (h r)"), slot_tab[:].rearrange("p h r -> p (h r)"),
                                  bk[:, 0:NCOL], ALU.add)

            def first_norm_stats(n):
                dve.wait_ge(xin_in, n * 16)
                for m in range(MB):
                    norm_stats(m, xin, var1 if m == MB - 1 else None)

            def first_norm(n):
                dve.wait_ge(std1, n)
                dve.reciprocal(first[:, 1, :], first[:, 0, :])
                dve.drain()
                dve.scalar_tensor_tensor(out=first[:, 2, :], in0=mv[:, :, 0], scalar=-1.0, in1=first[:, 1, :],
                                         op0=ALU.mult, op1=ALU.mult).then_inc(norm_known, 1)

            def finish(b, g):
                dve.wait_ge(pv_done, b * (NG * MB) + (g * MB + MB))
                dve.reciprocal(rec, bank[7][:])
                dve.drain()
                dve.tensor_tensor(attT[:, g, :], bank[6][:], rec, ALU.mult).then_inc(att_done, 1)

            def split_qk(b, m):
                for w, dst in enumerate((q16, k16)):
                    dve.wait_ge(qkT_sb, b * (2 * MB) + (2 * m + w + 1))
                    dve.tensor_tensor(dst[:, 1, :, m * P:m * P + P], qk32[:, w, :].rearrange("p (c n) -> p c n", c=4),
                                      dst[:, 0, :, m * P:m * P + P], ALU.subtract).then_inc(qk_lo, 1)

            def sequence(b, before):
                for m in range(MB):
                    dve.drain()
                    dve.wait_ge(qkv_ps, b * (3 * MB) + (3 * m + 2))
                    cos = C["rope_cos"][:, m * D:m * D + D].unsqueeze(1).to_broadcast([P, H, D])
                    for w in range(2):
                        ps, a1, a2 = heads(bank[w][:]), heads(t1[:, w * E:w * E + E]), heads(t2[:, w * E:w * E + E])
                        dve.tensor_tensor(a1, ps, cos, ALU.mult)
                        for h in range(2):
                            lo, hi = h * D // 2, (1 - h) * D // 2
                            sin = C["rope_sin"][:, m * D + lo:m * D + lo + D // 2].unsqueeze(1).to_broadcast([P, H, D // 2])
                            i = dve.tensor_tensor(a2[:, :, lo:lo + D // 2], ps[:, :, hi:hi + D // 2], sin, ALU.mult)
                    i.then_inc(rope_parts, 1)
                    dve.drain()
                    dve.tensor_tensor(t1, t1, t2, ALU.add)
                    dve.drain()
                    dve.tensor_reduce(hs[:, 0, :], heads(t1), AX_X, ALU.add)
                    dve.drain()
                    dve.tensor_scalar(hs[:, 0, :], hs[:, 0, :], 1.0 / D, None, ALU.mult)
                    dve.drain()
                    dve.tensor_tensor(heads(t1), heads(t1), per_head(hs[:, 0, :]), ALU.subtract).then_inc(centred, 1)
                    if m:
                        split_qk(b, m - 1)
                    dve.wait_ge(squares, b * MB + (m + 1))
                    dve.tensor_reduce(hs[:, 0, :], heads(t2), AX_X, ALU.add).then_inc(hvar, 1)
                    dve.wait_ge(hstd, b * MB + (m + 1))
                    dve.reciprocal(hs[:, 2, :], hs[:, 1, :])
                    dve.drain()
                    if m:
                        dve.wait_ge(qkT_ps, b * (2 * MB) + 2 * m)
                    dve.tensor_tensor(heads(qkn[:]), heads(t1), per_head(hs[:, 2, :]), ALU.mult).then_inc(qkn_ready, 1)

                split_qk(b, MB - 1)
                for i in range(NG * MB):
                    kb = i % MB
                    if i >= 2:
                        dve.wait_ge(pv_done, b * (NG * MB) + (i - 1))
                    for j in (0, 2):
                        dve.wait_ge(sq_done, b * (NG * MB * HG) + (HG * i + j + 1))
                        s2 = s_sq[:, j, 0:N - P * kb]
                        dve.tensor_tensor(s_p4[:, i % 2, j, 0:N - P * kb], s2, s2, ALU.mult).then_inc(p4_done[0], 1)
                    if i and kb == 0:
                        finish(b, i // MB - 1)
                    if before is not None:
                        if i == 1:
                            group_sums(before)
                        elif i == 2:
                            group_choice()
                        elif i == 3:
                            compare(mb[:], NX)
                        elif i == 4:
                            expert_choice()
                        elif i == 5:
                            choice_weights(before)
                        elif i == 6:
                            choice_values()
                        elif i == 8:
                            choice_places(before)
                        elif 9 <= i < 9 + MB:
                            place_rows(i - 9)
                    if i == 12:
                        first_norm_stats(b + 2)
                    if i == 14:
                        first_norm(b + 2)
                finish(b, NG - 1)
                if before is not None:
                    add_table(before)
                dve.wait_ge(xres_in, b * 16 + 16)
                for m in range(MB):
                    dve.wait_ge(proj_ps, b * MB + (m + 1))
                    dve.tensor_tensor(xres[:, m, :], xres[:, m, :], bank[m][:], ALU.add).then_inc(x1_ready, 1)
                dve.drain()
                for m in range(MB):
                    norm_stats(m, xres, var2 if m == MB - 1 else None)
                dve.wait_ge(std2, b + 1)
                normed(xn2, xres, xn2_ready)
                for m in range(MB):
                    dve.wait_ge(xhi_done, b * MB + (m + 1))
                    i = dve.scalar_tensor_tensor(out=xn16[:, m, 1, :], in0=xn2[:, m, :], scalar=XS, in1=xn16[:, m, 0, :],
                                                 op0=ALU.mult, op1=ALU.subtract)
                i.then_inc(xn16_ready, 1)

            first_norm_stats(1)
            first_norm(1)
            dve.wait_ge(consts_in, 16 * NCST)
            dve.wait_ge(memset_done, 1)
            dve.tensor_copy(ident16[:], C["ident16"][:])
            dve.tensor_scalar(ln_s[:], ln_s[:], QS, None, ALU.mult)
            dve.tensor_scalar(ln_b[:], ln_b[:], QS, None, ALU.mult)
            dve.wait_ge(weights_out, 16)
            dve.wait_ge(zeros_out, 16)
            sequence(0, None)
            with dve.Fori(0, B - 1) as r:
                sequence(r + 1, r)
            group_sums(B - 1)
            group_choice()

            def find_tiles():
                dve.wait_ge(count_ps, 1)
                nt, base = d16[:, 0, :], d16[:, 1, :]
                dve.tensor_scalar(nt, bank[7][:, 0:NX], float(P - 1), None, ALU.add)
                dve.drain()
                dve.tensor_copy(d16i[:, 0, :], nt)
                dve.drain()
                dve.tensor_scalar(d16i[:, 1, :], d16i[:, 0, :], P.bit_length() - 1, None, ALU.logical_shift_right)
                dve.drain()
                dve.tensor_copy(nt, d16i[:, 1, :])
                dve.drain()
                big = oh4[:, 0:NX * NX]
                dve.tensor_tensor(big.rearrange("p (e f) -> p e f", e=NX), nt.unsqueeze(1).to_broadcast([P, NX, NX]),
                                  C["tie16"][:].rearrange("p (e f) -> p e f", e=NX), ALU.mult)
                dve.drain()
                dve.tensor_reduce(base, big.rearrange("p (e f) -> p e f", e=NX), AX_X, ALU.add)
                dve.drain()
                hot = C["col_onehot"][:].rearrange("p (h e) -> p h e", h=CH)
                for i, v in enumerate((base, nt)):
                    o = oh4[:, i * CH * NX:(i + 1) * CH * NX].rearrange("p (h e) -> p h e", h=CH)
                    dve.tensor_tensor(o, hot, v.unsqueeze(1).to_broadcast([P, CH, NX]), ALU.mult)
                    dve.drain()
                    dve.tensor_reduce(d2[:, i, :], o, AX_X, ALU.add)
                dve.drain()
                dve.tensor_tensor(d2[:, 2, :], C["col_piece"][:], d2[:, 1, :], ALU.is_lt)
                dve.tensor_tensor(d2[:, 0, :], d2[:, 0, :], C["col_piece"][:], ALU.add)
                dve.drain()
                dve.scalar_tensor_tensor(out=d2[:, 0, :], in0=d2[:, 0, :], scalar=1.0, in1=d2[:, 2, :], op0=ALU.add, op1=ALU.mult)
                dve.drain()
                dve.tensor_scalar(d2[:, 0, :], d2[:, 0, :], -1.0, None, ALU.add)
                dve.drain()
                for h in range(CH):
                    k = dve.tensor_scalar(tile_hot[:, h, :], C["iota"][:, 0:RT], d2[:, 0, h:h + 1], None, ALU.is_equal)
                k.then_inc(tiles_known, 1)

            def find_rows():
                dve.wait_ge(ids_ps, 1)
                dve.tensor_scalar(free[:], bank[7][:, 0:RT], 0.0, C["free_row"][:, 0:1], ALU.is_equal, ALU.mult)
                dve.drain()
                dve.scalar_tensor_tensor(out=free[:], in0=bank[7][:, 0:RT], scalar=-1.0, in1=free[:],
                                         op0=ALU.add, op1=ALU.add)
                dve.tensor_copy(expert_id[:], bank[7][:, RT:2 * RT])
                dve.drain()
                dve.tensor_copy(row_id[:], free[:]).then_inc(ids_ready, 1)

            def routing(t):
                b = B - 1
                if t == 0:
                    compare(mb[:], NX)
                elif t == 1:
                    expert_choice()
                elif t == 2:
                    choice_weights(b)
                    choice_values()
                elif t == 3:
                    choice_places(b, bank[7])
                elif 4 <= t < 4 + MB:
                    place_rows(t - 4)
                elif t == 8:
                    add_table(b, bank[7])
                    dve.drain()
                    dve.engine_nop().then_inc(sel_ready, 1)
                elif t == 9:
                    find_tiles()
                elif t == 10:
                    find_rows()

            def hidden(t):
                k = t.par
                h, mx = hh[:, k], hsc[:, k, 0:1]
                dve.wait_ge(silu_done, t.at(1))
                dve.tensor_tensor(h, sg[:, k], bank[2 + k][:, FF:2 * FF], ALU.mult).then_inc(up_used, 1)
                dve.drain()
                dve.tensor_reduce(mx, h, AX_X, ALU.max, apply_absolute_value=True)
                dve.drain()
                dve.tensor_scalar(hsc[:, k, 1:2], mx, 1e-30, 1.0 / HMAX, ALU.max, ALU.mult)
                dve.drain()
                dve.reciprocal(hsc[:, k, 2:3], hsc[:, k, 1:2])
                back = 1.0 / (XS * WS * WS)
                if t.shared():
                    dve.tensor_scalar(hsc[:, k, 3:4], hsc[:, k, 1:2], back, None, ALU.mult)
                else:
                    dve.wait_ge(weights_here, t.at(1 - TB))
                    dve.tensor_scalar(hsc[:, k, 3:4], hsc[:, k, 1:2], back, wr[:, k:k + 1], ALU.mult, ALU.mult)
                dve.drain()
                if not t.below(2):
                    dve.wait_ge(hT_ps, t.at(-1))
                dve.tensor_scalar(h16[:, k, 0], h, hsc[:, k, 2:3], None, ALU.mult)
                dve.drain()
                dve.scalar_tensor_tensor(out=h16[:, k, 1], in0=h, scalar=hsc[:, k, 2:3], in1=h16[:, k, 0],
                                         op0=ALU.mult, op1=ALU.subtract).then_inc(h_ready, 1)

            def output(t):
                k = t.par
                if t.shared():
                    dve.wait_ge(x1r_in[k], t.uses() * 16)
                    if not t.below(2):
                        dve.wait_ge(fin_out[k], t.uses(-1) * 16)
                    dve.wait_ge(y_ps, t.at(1))
                    dve.scalar_tensor_tensor(out=yy[:, k], in0=bank[5 + k][:], scalar=hsc[:, k, 3:4], in1=x1r[:, k],
                                             op0=ALU.mult, op1=ALU.add).then_inc(y_sb, 1)
                    return
                if t.below(TB + 2):
                    dve.wait_ge(fin_out[k], 16 * TB // 2)
                else:
                    dve.wait_ge(added, t.at(-TB - 1) * 16)
                dve.wait_ge(y_ps, t.at(1))
                dve.tensor_scalar(yy[:, k], bank[5 + k][:], hsc[:, k, 3:4], None, ALU.mult).then_inc(y_sb, 1)

            def step(t):
                hidden(t)
                if not t.is_(0):
                    output(t.plus(-1))

            all_tiles(dve, step, routing)
            output(Tile(None, NT - 1))


def kernel(**inputs):
    import concourse.bacc as bacc
    from concourse.bass_utils import run_bass_kernel_spmd

    a = {k.replace("L0_", ""): np.asarray(v) for k, v in inputs.items()}
    put = np.ascontiguousarray
    gate = np.concatenate([a["ffn_shared_gate"][None], a["ffn_gate_proj"]])
    up = np.concatenate([a["ffn_shared_up"][None], a["ffn_up_proj"]])
    down = np.concatenate([a["ffn_shared_down"][None], a["ffn_down_proj"]])
    gu = np.concatenate([gate, up], 1).transpose(0, 2, 1).reshape(NX + 1, EC, P, 2 * FF)
    dn = down.transpose(0, 2, 1).reshape(NX + 1, FC, P, E)
    chunks = np.concatenate([gu, dn], 1).transpose(0, 2, 1, 3)
    arrays = {
        "x": put(a["attn_x"].reshape(B, MB, P, E).transpose(0, 2, 1, 3)),
        "w_qkv": put(a["attn_w_qkv"].reshape(EC, P, 3 * E).transpose(1, 0, 2)),
        "w_out": put(a["attn_w_out"].reshape(EC, P, E).transpose(1, 0, 2)),
        "ln_scale": put(np.tile(a["attn_ln_scale"], HG)[:, None]),
        "ln_bias": put(np.tile(a["attn_ln_bias"], HG)[:, None]),
        "gate_w": put(a["ffn_gate_weight"].T.reshape(EC, P, NX).transpose(1, 0, 2)),
        "expert_bias": put(np.tile(a["ffn_expert_bias"][None, :], (P, 1))),
        "w_experts": put(chunks.reshape(NX + 1, P, 2, HC * E)),
    }
    consts = constants()
    nc = bacc.Bacc("TRN2", target_bir_lowering=False, num_devices=1)
    dram = lambda n, v: nc.dram_tensor(n, v.shape, F32, kind="ExternalInput").ap()
    aps = {k: dram(k, v) for k, v in arrays.items()}
    cst = {k: dram("const_" + k, v) for k, v in consts.items()}
    out = nc.dram_tensor("out", (T + P, E), F32, kind="ExternalOutput").ap()
    build(nc, cst=cst, out=out, **aps)
    arrays.update({"const_" + k: v for k, v in consts.items()})
    r = run_bass_kernel_spmd(nc, [arrays], core_ids=[0])
    return r.results[0]["out"][0:T].reshape(B, N, E)
```
